# Optimizing a Trainium2 kernel written in Bass

```python
import numpy as np
import jax
import jax.numpy as jnp

def _softmax(x, axis=-1):
    return jax.nn.softmax(x, axis=axis)

def _gelu(x):
    return jax.nn.gelu(x, approximate=True)

def _silu(x):
    return jax.nn.silu(x)

def _sigmoid(x):
    return jax.nn.sigmoid(x)

def _layernorm(x, axis=-1, eps=1e-05):
    m = jnp.mean(x, axis=axis, keepdims=True)
    v = jnp.var(x, axis=axis, keepdims=True)
    return (x - m) / jnp.sqrt(v + eps)

def _scatter_add(tgt, idx, src, axis=0):
    return tgt.at[idx].add(src)

def _segment_sum(src, seg, n):
    return jax.ops.segment_sum(src, seg, n)
kernel_name = 'mk_sandwich_d2_jaxref_r8_be8f3e'

def setup_inputs(seed: int=0):
    np.random.seed(seed)
    _w = jnp.asarray

    def _L0_attn_setup():
        import jax, jax.numpy as jnp
        import numpy as np
        B, T, D, H = (1, 512, 128, 16)
        DK = D // H
        SCALE = 1.0 / float(np.sqrt(DK))
        NEG = -1000000000.0
        key = jax.random.key(seed)
        k1, k2, k3 = jax.random.split(key, 3)
        x = jax.random.normal(k1, (B, T, D), dtype=jnp.float32)
        Wqkv = jax.random.normal(k2, (3 * D, D), dtype=jnp.float32) * 0.02
        Wout = jax.random.normal(k3, (D, D), dtype=jnp.float32) * 0.02
        return {'x': x, 'Wqkv': Wqkv, 'Wout': Wout}
    _L0_attn_in = _L0_attn_setup()

    def _L0_ffn_setup():
        import jax, jax.numpy as jnp
        import numpy as np
        B, T, C = (2, 256, 128)
        H, D = (16, 64)
        CR = 8
        R = C // CR
        ROPE = D // 2
        NOPE = D - ROPE
        E, K, I, S = (8, 2, 64, 1)
        THETA = 100000.0
        EPS = 1e-05

        def _rmsnorm(x, w):
            rms = jnp.sqrt(jnp.mean(x * x, axis=-1, keepdims=True) + EPS)
            return w * (x / rms)

        def _rope(xh):
            d = xh.shape[-1]
            t = jnp.arange(xh.shape[2], dtype=jnp.float32)
            freqs = 1.0 / THETA ** (jnp.arange(0, d, 2, dtype=jnp.float32) / d)
            ang = jnp.outer(t, freqs)
            cos, sin = (jnp.cos(ang), jnp.sin(ang))
            xr = xh.reshape(xh.shape[:-1] + (d // 2, 2))
            x0, x1 = (xr[..., 0], xr[..., 1])
            rot = jnp.stack([x0 * cos - x1 * sin, x0 * sin + x1 * cos], axis=-1)
            return rot.reshape(xh.shape)

        def _attention(x, Wq, Wkva, Wkvb, Wo):
            b, t, _ = x.shape
            q = (x @ Wq).reshape(b, t, H, D).transpose(0, 2, 1, 3)
            ckv = x @ Wkva
            kv_latent, k_rope = (ckv[:, :, :R], ckv[:, :, R:])
            kv = (kv_latent @ Wkvb).reshape(b, t, H, NOPE).transpose(0, 2, 1, 3)
            k_rope = jnp.broadcast_to(k_rope[:, None, :, :], (b, H, t, ROPE))
            q_nope, q_rope = (q[..., :NOPE], q[..., NOPE:])
            q = jnp.concatenate([q_nope, _rope(q_rope)], axis=-1)
            k = jnp.concatenate([kv, _rope(k_rope)], axis=-1)
            v = jnp.concatenate([kv, jnp.zeros_like(k_rope)], axis=-1)
            att = jnp.einsum('bhqd,bhkd->bhqk', q, k) / jnp.sqrt(jnp.float32(D))
            mask = jnp.tril(jnp.ones((t, t), dtype=bool))
            att = jnp.where(mask, att, jnp.float32(-jnp.inf))
            att = jax.nn.softmax(att, axis=-1)
            y = jnp.einsum('bhqk,bhkd->bhqd', att, v)
            y = y.transpose(0, 2, 1, 3).reshape(b, t, H * D)
            return y @ Wo

        def _experts(x_flat, Wg, Wu, Wd):
            g = jax.nn.silu(jnp.einsum('nc,eci->nei', x_flat, Wg))
            u = jnp.einsum('nc,eci->nei', x_flat, Wu)
            return jnp.einsum('nei,eic->nec', g * u, Wd)

        def _moe(x, Wgate, expert_bias, Wg, Wu, Wd, sWg, sWu, sWd):
            b, t, c = x.shape
            xf = x.reshape(-1, c)
            shared = jnp.mean(_experts(xf, sWg, sWu, sWd), axis=1)
            logits = xf @ Wgate + expert_bias
            probs = jax.nn.softmax(logits, axis=-1)
            topk_p, topk_i = jax.lax.top_k(probs, K)
            topk_p = topk_p / jnp.sum(topk_p, axis=-1, keepdims=True)
            comb = jnp.sum(jax.nn.one_hot(topk_i, E, dtype=xf.dtype) * topk_p[..., None], axis=1)
            routed = jnp.einsum('ne,nec->nc', comb, _experts(xf, Wg, Wu, Wd))
            return (shared + routed).reshape(b, t, c)
        key = jax.random.key(seed)
        ks = jax.random.split(key, 16)
        w = lambda k, shp: jax.random.normal(k, shp, dtype=jnp.float32) * 0.02
        return {'x': jax.random.normal(ks[0], (B, T, C), dtype=jnp.float32), 'w_ln1': jnp.ones((C,), jnp.float32), 'Wq': w(ks[1], (C, H * D)), 'Wkva': w(ks[2], (C, R + ROPE)), 'Wkvb': w(ks[3], (R, H * NOPE)), 'Wo': w(ks[4], (H * D, C)), 'w_ln2': jnp.ones((C,), jnp.float32), 'Wgate': w(ks[5], (C, E)), 'expert_bias': jnp.zeros((E,), jnp.float32), 'Wg': w(ks[6], (E, C, I)), 'Wu': w(ks[7], (E, C, I)), 'Wd': w(ks[8], (E, I, C)), 'sWg': w(ks[9], (S, C, I)), 'sWu': w(ks[10], (S, C, I)), 'sWd': w(ks[11], (S, I, C))}
    _L0_ffn_in = _L0_ffn_setup()

    def _L1_attn_setup():
        import jax, jax.numpy as jnp
        import numpy as np
        N_HEAD = 16
        key = jax.random.key(seed)
        k1, k2 = jax.random.split(key)
        B, T, C = (4, 256, 128)
        x = jax.random.normal(k1, (B, T, C), dtype=jnp.float32)
        w_qkv = jax.random.normal(k2, (C, 3 * C), dtype=jnp.float32) * (1.0 / np.sqrt(C))
        return {'x': x, 'w_qkv': w_qkv}
    _L1_attn_in = _L1_attn_setup()

    def _L1_ffn_setup():
        import jax, jax.numpy as jnp
        import numpy as np
        D_MODEL, D_FF, RANK = (128, 512, 32)
        B, S = (4, 512)
        key = jax.random.key(seed)
        ks = jax.random.split(key, 7)
        return {'x': jax.random.normal(ks[0], (B, S, D_MODEL), dtype=jnp.float32), 'U1': jax.random.normal(ks[1], (D_MODEL, RANK), dtype=jnp.float32) * 0.02, 'V1': jax.random.normal(ks[2], (RANK, D_FF), dtype=jnp.float32) * 0.02, 'b1': jnp.zeros((D_FF,), dtype=jnp.float32), 'U2': jax.random.normal(ks[3], (D_FF, RANK), dtype=jnp.float32) * 0.02, 'V2': jax.random.normal(ks[4], (RANK, D_MODEL), dtype=jnp.float32) * 0.02, 'b2': jnp.zeros((D_MODEL,), dtype=jnp.float32)}
    _L1_ffn_in = _L1_ffn_setup()
    _d = {'L0_attn_x': _L0_attn_in['x'], 'L0_attn_Wqkv': _L0_attn_in['Wqkv'], 'L0_attn_Wout': _L0_attn_in['Wout'], 'L0_ffn_w_ln1': _L0_ffn_in['w_ln1'], 'L0_ffn_Wq': _L0_ffn_in['Wq'], 'L0_ffn_Wkva': _L0_ffn_in['Wkva'], 'L0_ffn_Wkvb': _L0_ffn_in['Wkvb'], 'L0_ffn_Wo': _L0_ffn_in['Wo'], 'L0_ffn_w_ln2': _L0_ffn_in['w_ln2'], 'L0_ffn_Wgate': _L0_ffn_in['Wgate'], 'L0_ffn_expert_bias': _L0_ffn_in['expert_bias'], 'L0_ffn_Wg': _L0_ffn_in['Wg'], 'L0_ffn_Wu': _L0_ffn_in['Wu'], 'L0_ffn_Wd': _L0_ffn_in['Wd'], 'L0_ffn_sWg': _L0_ffn_in['sWg'], 'L0_ffn_sWu': _L0_ffn_in['sWu'], 'L0_ffn_sWd': _L0_ffn_in['sWd'], 'L1_attn_w_qkv': _L1_attn_in['w_qkv'], 'L1_ffn_U1': _L1_ffn_in['U1'], 'L1_ffn_V1': _L1_ffn_in['V1'], 'L1_ffn_b1': _L1_ffn_in['b1'], 'L1_ffn_U2': _L1_ffn_in['U2'], 'L1_ffn_V2': _L1_ffn_in['V2'], 'L1_ffn_b2': _L1_ffn_in['b2']}
    _x0 = _d['L0_attn_x']
    _d['L0_attn_x'] = jax.random.normal(jax.random.fold_in(jax.random.key(seed), 1), (4, 1024, 128), dtype=_x0.dtype)
    del _x0
    return _d

def reference(L0_attn_x, L0_attn_Wqkv, L0_attn_Wout, L0_ffn_w_ln1, L0_ffn_Wq, L0_ffn_Wkva, L0_ffn_Wkvb, L0_ffn_Wo, L0_ffn_w_ln2, L0_ffn_Wgate, L0_ffn_expert_bias, L0_ffn_Wg, L0_ffn_Wu, L0_ffn_Wd, L0_ffn_sWg, L0_ffn_sWu, L0_ffn_sWd, L1_attn_w_qkv, L1_ffn_U1, L1_ffn_V1, L1_ffn_b1, L1_ffn_U2, L1_ffn_V2, L1_ffn_b2):

    def _L0_attn_ref(x, Wqkv, Wout):
        import jax, jax.numpy as jnp
        import numpy as np
        B, T, D, H = (1, 512, 128, 16)
        DK = D // H
        SCALE = 1.0 / float(np.sqrt(DK))
        NEG = -1000000000.0
        b, t, d = x.shape
        qkv = jnp.einsum('btd,ed->bte', x, Wqkv)
        qkv = qkv.reshape(b, t, 3, H, DK).transpose(2, 0, 3, 1, 4)
        q, k, v = (qkv[0], qkv[1], qkv[2])
        scores = jnp.einsum('bhtd,bhsd->bhts', q, k) * SCALE
        scores = jnp.clip(scores, -10.0, 10.0)
        mask = jnp.triu(jnp.full((t, t), NEG, dtype=scores.dtype), k=1)
        scores = scores + mask[None, None, :, :]
        attn = jax.nn.softmax(scores, axis=-1)
        out = jnp.einsum('bhts,bhsd->bhtd', attn, v)
        out = out.transpose(0, 2, 1, 3).reshape(b, t, d)
        return jnp.einsum('btd,ed->bte', out, Wout)

    def _L0_ffn_ref(x, w_ln1, Wq, Wkva, Wkvb, Wo, w_ln2, Wgate, expert_bias, Wg, Wu, Wd, sWg, sWu, sWd):
        import jax, jax.numpy as jnp
        import numpy as np
        B, T, C = (2, 256, 128)
        H, D = (16, 64)
        CR = 8
        R = C // CR
        ROPE = D // 2
        NOPE = D - ROPE
        E, K, I, S = (8, 2, 64, 1)
        THETA = 100000.0
        EPS = 1e-05

        def _rmsnorm(x, w):
            rms = jnp.sqrt(jnp.mean(x * x, axis=-1, keepdims=True) + EPS)
            return w * (x / rms)

        def _rope(xh):
            d = xh.shape[-1]
            t = jnp.arange(xh.shape[2], dtype=jnp.float32)
            freqs = 1.0 / THETA ** (jnp.arange(0, d, 2, dtype=jnp.float32) / d)
            ang = jnp.outer(t, freqs)
            cos, sin = (jnp.cos(ang), jnp.sin(ang))
            xr = xh.reshape(xh.shape[:-1] + (d // 2, 2))
            x0, x1 = (xr[..., 0], xr[..., 1])
            rot = jnp.stack([x0 * cos - x1 * sin, x0 * sin + x1 * cos], axis=-1)
            return rot.reshape(xh.shape)

        def _attention(x, Wq, Wkva, Wkvb, Wo):
            b, t, _ = x.shape
            q = (x @ Wq).reshape(b, t, H, D).transpose(0, 2, 1, 3)
            ckv = x @ Wkva
            kv_latent, k_rope = (ckv[:, :, :R], ckv[:, :, R:])
            kv = (kv_latent @ Wkvb).reshape(b, t, H, NOPE).transpose(0, 2, 1, 3)
            k_rope = jnp.broadcast_to(k_rope[:, None, :, :], (b, H, t, ROPE))
            q_nope, q_rope = (q[..., :NOPE], q[..., NOPE:])
            q = jnp.concatenate([q_nope, _rope(q_rope)], axis=-1)
            k = jnp.concatenate([kv, _rope(k_rope)], axis=-1)
            v = jnp.concatenate([kv, jnp.zeros_like(k_rope)], axis=-1)
            att = jnp.einsum('bhqd,bhkd->bhqk', q, k) / jnp.sqrt(jnp.float32(D))
            mask = jnp.tril(jnp.ones((t, t), dtype=bool))
            att = jnp.where(mask, att, jnp.float32(-jnp.inf))
            att = jax.nn.softmax(att, axis=-1)
            y = jnp.einsum('bhqk,bhkd->bhqd', att, v)
            y = y.transpose(0, 2, 1, 3).reshape(b, t, H * D)
            return y @ Wo

        def _experts(x_flat, Wg, Wu, Wd):
            g = jax.nn.silu(jnp.einsum('nc,eci->nei', x_flat, Wg))
            u = jnp.einsum('nc,eci->nei', x_flat, Wu)
            return jnp.einsum('nei,eic->nec', g * u, Wd)

        def _moe(x, Wgate, expert_bias, Wg, Wu, Wd, sWg, sWu, sWd):
            b, t, c = x.shape
            xf = x.reshape(-1, c)
            shared = jnp.mean(_experts(xf, sWg, sWu, sWd), axis=1)
            logits = xf @ Wgate + expert_bias
            probs = jax.nn.softmax(logits, axis=-1)
            topk_p, topk_i = jax.lax.top_k(probs, K)
            topk_p = topk_p / jnp.sum(topk_p, axis=-1, keepdims=True)
            comb = jnp.sum(jax.nn.one_hot(topk_i, E, dtype=xf.dtype) * topk_p[..., None], axis=1)
            routed = jnp.einsum('ne,nec->nc', comb, _experts(xf, Wg, Wu, Wd))
            return (shared + routed).reshape(b, t, c)
        x = x + _attention(_rmsnorm(x, w_ln1), Wq, Wkva, Wkvb, Wo)
        residual = x
        xn = _rmsnorm(x, w_ln2)
        x_out = _moe(xn, Wgate, expert_bias, Wg, Wu, Wd, sWg, sWu, sWd)
        return residual + x_out

    def _L1_attn_ref(x, w_qkv):
        import jax, jax.numpy as jnp
        import numpy as np
        N_HEAD = 16
        B, T, C = x.shape
        H = N_HEAD
        D = C // H
        qkv = x @ w_qkv
        q, k, v = jnp.split(qkv, 3, axis=2)
        q = q.reshape(B, T, H, D).transpose(0, 2, 1, 3)
        k = k.reshape(B, T, H, D).transpose(0, 2, 1, 3)
        v = v.reshape(B, T, H, D).transpose(0, 2, 1, 3)
        scale = np.float32(1.0 / np.sqrt(D))
        att = jnp.einsum('bhqd,bhkd->bhqk', q, k) * scale
        causal = jnp.tril(jnp.ones((T, T), dtype=bool))
        att = jnp.where(causal, att, -jnp.inf)
        att = jax.nn.softmax(att, axis=-1)
        out = jnp.einsum('bhqk,bhkd->bhqd', att, v)
        return out.transpose(0, 2, 1, 3).reshape(B, T, C)

    def _L1_ffn_ref(x, U1, V1, b1, U2, V2, b2):
        import jax, jax.numpy as jnp
        import numpy as np
        D_MODEL, D_FF, RANK = (128, 512, 32)
        B, S = (4, 512)
        P = jnp.einsum('bsd,dr->bsr', x, U1)
        H = jax.nn.gelu(jnp.einsum('bsr,rf->bsf', P, V1) + b1)
        Q = jnp.einsum('bsf,fr->bsr', H, U2)
        return jnp.einsum('bsr,rd->bsd', Q, V2) + b2
    x = L0_attn_x
    x = x + _layernorm(_L0_attn_ref(_layernorm(x, axis=-1), L0_attn_Wqkv, L0_attn_Wout), axis=-1)
    x = x + _layernorm(_L0_ffn_ref(_layernorm(x, axis=-1), L0_ffn_w_ln1, L0_ffn_Wq, L0_ffn_Wkva, L0_ffn_Wkvb, L0_ffn_Wo, L0_ffn_w_ln2, L0_ffn_Wgate, L0_ffn_expert_bias, L0_ffn_Wg, L0_ffn_Wu, L0_ffn_Wd, L0_ffn_sWg, L0_ffn_sWu, L0_ffn_sWd), axis=-1)
    x = x + _layernorm(_L1_attn_ref(_layernorm(x, axis=-1), L1_attn_w_qkv), axis=-1)
    x = x + _layernorm(_L1_ffn_ref(_layernorm(x, axis=-1), L1_ffn_U1, L1_ffn_V1, L1_ffn_b1, L1_ffn_U2, L1_ffn_V2, L1_ffn_b2), axis=-1)
    return x

_drawn_inputs = setup_inputs


def setup_inputs(seed=0):
    import zlib

    import numpy as np

    out = dict(_drawn_inputs(seed))
    spreads = {'L0_ffn_w_ln1': (1.0, 0.6),
     'L0_ffn_w_ln2': (1.0, 0.6),
     'L0_ffn_expert_bias': (0.0, 0.8),
     'L1_ffn_b1': (0.0, 0.8),
     'L1_ffn_b2': (0.0, 0.331)}
    factors = {'L0_ffn_Wq': 8.0,
     'L0_ffn_Wkva': 8.0,
     'L0_ffn_Wkvb': 8.0,
     'L0_ffn_Wo': 8.0,
     'L0_ffn_Wgate': 8.0,
     'L0_ffn_Wg': 8.0,
     'L0_ffn_Wu': 8.0,
     'L0_ffn_Wd': 8.0,
     'L0_ffn_sWg': 8.0,
     'L0_ffn_sWu': 8.0,
     'L0_ffn_sWd': 8.0,
     'L1_ffn_U1': 8.0,
     'L1_ffn_V1': 8.0,
     'L1_ffn_U2': 5.726,
     'L1_ffn_V2': 6.014}
    for name, (base, spread) in spreads.items():
        noise = np.random.default_rng([zlib.crc32(name.encode()), seed]).standard_normal(out[name].shape)
        drawn = base * np.exp(spread * noise) if base else spread * noise
        out[name] = jnp.asarray(drawn.astype(out[name].dtype))
    for name, factor in factors.items():
        out[name] = (out[name] * factor).astype(out[name].dtype)
    return out
```

```python
from contextlib import ExitStack

import concourse.bass as bass
from concourse import mybir
import numpy as np

P = 128
F32 = mybir.dt.float32
BF16 = mybir.dt.bfloat16
ALU = mybir.AluOpType
ACT = mybir.ActivationFunctionType
AX_X = mybir.AxisListType.X

BATCH, T, C = 4, 1024, 128
TOK = BATCH * T
TILES = TOK // P
CH = 512
CT = CH // P
HALVES = T // CH
KB = T // P
HEADS, QUAD = 16, 4
NQ = HEADS // QUAD
ITEMS = BATCH * NQ
UNIT = CH
ROWS_P = (KB * (KB + 1) // 2) * P // UNIT
UNITS = ROWS_P * QUAD
VW = 32
EPS = 1e-5
BASE = 1
NEG = -1e30
QTERM = (0, 0, 0, 1, 1, 2)
KTERM = (0, 1, 2, 0, 1, 0)
LAT, ROPE, MD = 16, 32, 48
EXPERTS, TOPK, INNER = 8, 2, 64
PAIRS = EXPERTS // 2
RANK, DFF = 32, 512


def key_major_units():
    blocks = [(k, q) for k in range(KB) for q in range(k, KB)]
    units = []
    for g in range(ROWS_P):
        segs = []
        for off, (k, q) in enumerate(blocks[4 * g:4 * g + 4]):
            if segs and segs[-1][0] == k:
                segs[-1][2] += 1
            else:
                segs.append([k, q, 1, off])
        units.append([tuple(s) for s in segs])
    return units


def query_major_units():
    order = []
    for q in range(KB - 1, KB // 2 - 1, -1):
        order.append(q)
        if q > KB // 2:
            pass
    blocks = []
    for q in [7, 3, 6, 0, 5, 1, 4, 2]:
        blocks += [(q, k) for k in range(q + 1)]
    units = []
    for g in range(ROWS_P):
        segs = []
        for off, (q, k) in enumerate(blocks[4 * g:4 * g + 4]):
            if segs and segs[-1][0] == q:
                segs[-1][2] += 1
            else:
                segs.append([q, k, 1, off, 1 if k >= 4 else 0])
        units.append([tuple(s) for s in segs])
    return units


S_UNITS = key_major_units()
M_UNITS = query_major_units()


def build(nc, ins, consts, out):
    stack = ExitStack()
    with stack:
        def sb(name, shape, dt=F32):
            return stack.enter_context(nc.sbuf_tensor(name, shape, dt))

        phase_sems = []

        def sem(name):
            phase_sems.append(nc.alloc_semaphore(name=name))
            nc.sync.sem_inc(phase_sems[-1], BASE)
            return phase_sems[-1]

        def end_phase():
            nc.clear_and_free_semaphores(phase_sems)
            phase_sems.clear()
            nc.all_engine_barrier()

        def scratch(name, shape, dt=F32):
            return nc.dram_tensor(name, shape, dt, kind="Internal").ap()

        def wait_alone(eng, semaphore, value, *others):
            pairs = [(x, v + BASE if isinstance(v, int) else eng.to_reg(v + BASE))
                     for x, v in ((semaphore, value), *others)]
            eng.wait_ge(semaphore, BASE + 1)
            for x, v in pairs:
                eng.wait_ge(x, v)

        q8_d = scratch("q8_d", [ITEMS, 2, 3, 8, 2, T], BF16)
        k8_d = scratch("k8_d", [ITEMS, 2, 3, 8, 2, T], BF16)
        v8_d = scratch("v8_d", [TOK, HEADS * VW])
        qm_d = scratch("qm_d", [ITEMS, 3, MD, QUAD, T], BF16)
        km_d = scratch("km_d", [BATCH, 3, MD, T], BF16)
        vm_d = scratch("vm_d", [TOK, VW])
        mx_d = scratch("mx_d", [ITEMS, 3, QUAD, T], BF16)
        o_d = scratch("o_d", [ITEMS, P, T])
        xx_d = scratch("xx_d", [TOK, C])

        x_res = sb("x_res", [P, TILES, C])
        identity = sb("identity", [P, P])
        ident_bf = sb("ident_bf", [P, P], BF16)
        causal_bf = sb("causal_bf", [P, P], BF16)
        zero_f = sb("zero_f", [P, P])
        minus_half = sb("minus_half", [P, CT])

        FOLDED = ("wq_nope", "wkvb_z", "wo_nope")
        TABLES = ("cos_q", "sin_q", "cos_k", "sin_k")
        w_sb = {n: sb("w_" + n, list(a.shape)) for n, a in consts.items() if n not in FOLDED + TABLES}
        wabs = sb("wabs", [C, NQ // 2, 2, LAT, QUAD])
        wout_m = sb("wout_m", [P, 2, C])
        ps = stack.enter_context(nc.psum_tensor("ps", [P, 8, UNIT], F32))

        pmax = sb("pmax", [P, QUAD, KB, 2])
        mx_sb = sb("mx_sb", [P, 2, QUAD * KB])
        MR = QUAD * KB
        mx_turned = sb("mx_turned", [P, MR])
        m_parts = sb("m_parts", [P, 2, 3, MR], BF16)
        m_rest = sb("m_rest", [P, MR])
        o_sb = sb("o_sb", [P, 1, T])
        kterm_d = [scratch(f"kterm{c}_d", [BATCH, 2 * MD, T], BF16) for c in range(3)]

        ctx = dict(nc=nc, sb=sb, sem=sem, ps=ps, stack=stack)
        NB = 4
        q_buf = sb("q_buf", [P, NB, 3 * QUAD * T], BF16)
        k_buf = sb("k_buf", [P, NB, 3 * T], BF16)
        v_buf = sb("v_buf", [P, NB, KB * QUAD * VW])
        pr_buf = sb("pr_buf", [P, 12, UNIT])
        area = q_buf[:, :, :].rearrange("p a b -> p (a b)").bitcast(F32)
        area_at = [0]

        def work(*shape, dt=F32, parts=P):
            n = int(np.prod(shape))
            words = n if dt == F32 else (n + 1) // 2
            a = area[0:parts, area_at[0]:area_at[0] + words]
            area_at[0] += words
            assert area_at[0] <= 24576
            if dt != F32:
                a = a.bitcast(dt)
            names = "abcde"[:len(shape)]
            if len(shape) > 1:
                a = a.rearrange("p (" + " ".join(names) + ") -> p " + " ".join(names),
                                **{k: v for k, v in zip(names[1:], shape[1:])})
            return a

        for n in FOLDED:
            w_sb[n] = work(HEADS, P, parts=32)
        ld_w = sem("ld_w")
        c_zero = sem("c_zero")
        c_const = sem("c_const")
        c_bf = sem("c_bf")
        fold_mm = sem("fold_mm")
        with nc.Block() as block:
            @block.sync
            def _(sp):
                sp.dma_start(x_res[:, :, :], ins["x"].rearrange("b (t p) c -> p (b t) c", p=P)).then_inc(ld_w, 16)
                for n, w in w_sb.items():
                    sp.dma_start(w[tuple(slice(None) for _ in w.shape)], consts[n]).then_inc(ld_w, 16)
                sp.wait_ge(ld_w, 16 * (1 + len(w_sb)) + BASE)

            @block.gpsimd
            def _(pool):
                nc.gpsimd.memset(zero_f[:, :], 0.0).then_inc(c_zero, 1)
                nc.gpsimd.memset(minus_half[:, :], -0.5).then_inc(c_const, 1)
                pool.wait_ge(c_zero, 1 + BASE)
                nc.gpsimd.affine_select(out=identity[:, :], in_=zero_f[:, :], compare_op=ALU.not_equal, fill=1.0,
                                        base=0, pattern=[[-1, P]], channel_multiplier=1).then_inc(c_const, 1)
                pool.wait_ge(c_const, 2 + BASE)
                nc.gpsimd.tensor_copy(ident_bf[:, :], identity[:, :]).then_inc(c_const, 1)
                nc.gpsimd.affine_select(out=zero_f[:, :], in_=zero_f[:, :], compare_op=ALU.is_ge, fill=NEG,
                                        base=0, pattern=[[-1, P]], channel_multiplier=1).then_inc(c_const, 1)
                pool.wait_ge(c_const, 4 + BASE)
                nc.gpsimd.tensor_copy(causal_bf[:, :], zero_f[:, :]).then_inc(c_bf, 1)

            @block.tensor
            def _(pe):
                pe.wait_ge(ld_w, 16 * (1 + len(w_sb)) + BASE)
                for h in range(HEADS):
                    mm = nc.tensor.matmul(ps[:, 0, h * LAT:(h + 1) * LAT], w_sb["wq_nope"][:, h, :],
                                          w_sb["wkvb_z"][:, h, (h % 8) * LAT:(h % 8 + 1) * LAT],
                                          start=True, stop=True)
                mm.then_inc(fold_mm, 1)
                for half in range(2):
                    for h in range(8):
                        hh = 8 * half + h
                        mm = nc.tensor.matmul(ps[:, 1 + half, 0:C], w_sb["wkvb_z"][:, hh, :],
                                              w_sb["wo_nope"][:, hh, :], start=(h == 0), stop=(h == 7))
                mm.then_inc(fold_mm, 1)

            @block.vector
            def _(dve):
                dve.wait_ge(fold_mm, 1 + BASE)
                for half in range(2):
                    for qd in range(2):
                        nc.vector.tensor_copy(
                            wabs[:, half, qd, :, :],
                            ps[:, 0, (half * 8 + qd * 4) * LAT:(half * 8 + qd * 4 + 4) * LAT]
                            .rearrange("p (h r) -> p r h", h=QUAD))
                dve.wait_ge(fold_mm, 2 + BASE)
                nc.vector.tensor_copy(wout_m[:, 0, :], ps[:, 1, 0:C])
                nc.vector.tensor_copy(wout_m[:, 1, :], ps[:, 2, 0:C])

        def tiles_of(res, b, u):
            return res[:, bass.ds((b * HALVES + u) * CT, CT), :]

        class Norm:

            def __init__(self, name):
                self.bn = work(2, CT, 6)
                self.mv = work(2, CT, 2)
                self.ve = work(2, CT)
                self.rstd = work(2, CT)
                self.s_bn = sem(name + "_bn")
                self.s_mv = sem(name + "_mv")
                self.s_ve = sem(name + "_ve")
                self.s_rstd = sem(name + "_rstd")
                self.s_out = sem(name + "_out")

            def stats(self, dve, b, u, src):
                dve.wait_ge(self.s_ve, 2 * b + BASE)
                for t in range(CT):
                    i = nc.vector.bn_stats(self.bn[:, u, t, :], src[:, t, :])
                i.then_inc(self.s_bn, 1)
                wait_alone(dve, self.s_bn, 2 * b + u + 1)
                for t in range(CT):
                    i = nc.vector.bn_aggr(self.mv[:, u, t, :], self.bn[:, u, t, :])
                i.then_inc(self.s_mv, 1)

            def inverse(self, pool, b, u):
                wait_alone(pool, self.s_mv, 2 * b + u + 1, (self.s_out, 2 * b))
                nc.gpsimd.tensor_scalar(self.ve[:, u, :], self.mv[:, u, :, 1], EPS, None, ALU.add).then_inc(self.s_ve, 1)
                pool.wait_ge(self.s_ve, 2 * b + u + 1 + BASE)
                nc.gpsimd.tensor_tensor(self.rstd[:, u, :], self.ve[:, u, :], minus_half[:, :], ALU.pow)\
                    .then_inc(self.s_rstd, 1)

            def apply(self, dve, b, u, src, dst):
                dve.wait_ge(self.s_rstd, 2 * b + u + 1 + BASE)
                for t in range(CT):
                    i = nc.vector.tensor_scalar(dst[:, t, :], src[:, t, :], self.mv[:, u, t, 0:1],
                                                self.rstd[:, u, t:t + 1], ALU.subtract, ALU.mult)
                i.then_inc(self.s_out, 1)

        class RootMean:

            def __init__(self, name):
                self.junk = work(2, CT, C)
                self.ms = work(2, CT)
                self.ve = work(2, CT)
                self.rinv = work(2, CT)
                self.s_go = sem(name + "_go")
                self.s_ms = sem(name + "_ms")
                self.s_ve = sem(name + "_ve")
                self.s_rinv = sem(name + "_rinv")
                self.s_out = sem(name + "_out")

            def squares(self, act, b, u, src):
                used = act.to_reg(2 * b + BASE)
                act.wait_ge(self.s_go, 1 + BASE)
                act.wait_ge(self.s_ve, used)
                for t in range(CT):
                    i = nc.scalar.activation(self.junk[:, u, t, :], src[:, t, :], ACT.Square, scale=float(C) ** -0.5,
                                             accum_out=self.ms[:, u, t:t + 1])
                i.then_inc(self.s_ms, 1)

            def inverse(self, pool, b, u):
                wait_alone(pool, self.s_ms, 2 * b + u + 1, (self.s_out, 2 * b))
                nc.gpsimd.tensor_scalar(self.ve[:, u, :], self.ms[:, u, :], EPS, None, ALU.add).then_inc(self.s_ve, 1)
                pool.wait_ge(self.s_ve, 2 * b + u + 1 + BASE)
                nc.gpsimd.tensor_tensor(self.rinv[:, u, :], self.ve[:, u, :], minus_half[:, :], ALU.pow)\
                    .then_inc(self.s_rinv, 1)

            def apply(self, act, b, u, src, dst, dst_free):
                wait_alone(act, self.s_rinv, 2 * b + u + 1, dst_free)
                for t in range(CT):
                    i = nc.scalar.activation(dst[:, t, :], src[:, t, :], ACT.Copy, scale=self.rinv[:, u, t:t + 1])
                i.then_inc(self.s_out, 1)

        def transpose_chunk(bank, src):
            for t in range(CT):
                i = nc.tensor.transpose(ps[:, bank, t * P:(t + 1) * P], src[:, t, :], identity[:, :])
            return i

        def project_heads8(name, wq, wk, wv):
            area_at[0] = 0
            norm = Norm(name + "ln")
            xn = work(2, CT, C)
            xnT = work(2, CH)
            rest = work(2, 2, CH)
            parts = work(2, 2, 3, CH, dt=BF16)
            v_pad = work(2, CT, HEADS, VW)
            s_pad = sem(name + "_pad")
            s_T = sem(name + "_T")
            s_xT = sem(name + "_xT")
            s_qk = sem(name + "_qk")
            s_v = sem(name + "_v")
            s_p1 = sem(name + "_p1")
            s_r1 = sem(name + "_r1")
            s_p2 = sem(name + "_p2")
            s_p3 = sem(name + "_p3")
            s_vp = sem(name + "_vp")
            s_st = [sem(name + f"_st{u}") for u in range(2)]
            with nc.Block() as block:
                @block.vector
                def _(dve):
                    nc.vector.memset(v_pad, 0.0).then_inc(s_pad, 1)
                    dve.wait_ge(s_pad, 1 + BASE)
                    nc.vector.memset(v_pad[:, :, :, :, 8:9], 1.0).then_inc(s_pad, 1)
                    with dve.Fori(0, BATCH) as b:
                        for u in range(2):
                            norm.stats(dve, b, u, tiles_of(x_res, b, u))
                        for u in range(2):
                            dve.wait_ge(s_T, 2 * b + BASE)
                            norm.apply(dve, b, u, tiles_of(x_res, b, u), xn[:, u, :, :])
                        for u in range(2):
                            dve.wait_ge(s_p3, 4 * b + BASE)
                            for s in range(2):
                                dve.wait_ge(s_p1, 4 * b + 2 * u + s + 1 + BASE)
                                nc.vector.tensor_tensor(rest[:, u, s, :], ps[:, 2 + 2 * s + u, :],
                                                        parts[:, u, s, 0, :], ALU.subtract).then_inc(s_r1, 1)
                            dve.wait_ge(s_v, 2 * b + u + 1 + BASE)
                            dve.wait_ge(s_st[u], 16 * 7 * b + BASE)
                            nc.vector.tensor_copy(v_pad[:, u, :, :, 0:8],
                                                  ps[:, 6 + u, :].rearrange("p (t h d) -> p t h d", t=CT, h=HEADS))\
                                .then_inc(s_vp, 1)

                @block.gpsimd
                def _(pool):
                    with pool.Fori(0, BATCH) as b:
                        for u in range(2):
                            norm.inverse(pool, b, u)
                        for u in range(2):
                            for s in range(2):
                                pool.wait_ge(s_p2, 4 * b + 2 * u + s + 1 + BASE)
                                nc.gpsimd.tensor_tensor(parts[:, u, s, 2, :], rest[:, u, s, :], parts[:, u, s, 1, :],
                                                        ALU.subtract).then_inc(s_p3, 1)

                @block.tensor
                def _(pe):
                    with pe.Fori(0, BATCH) as b:
                        for u in range(2):
                            pe.wait_ge(norm.s_out, 2 * b + u + 1 + BASE)
                            pe.wait_ge(s_xT, 2 * b + BASE)
                            transpose_chunk(u, xn[:, u, :, :]).then_inc(s_T, 1)
                        for u in range(2):
                            pe.wait_ge(s_xT, 2 * b + u + 1 + BASE)
                            pe.wait_ge(s_r1, 4 * b + BASE)
                            for s, w in enumerate((wq, wk)):
                                nc.tensor.matmul(ps[:, 2 + 2 * s + u, :], w, xnT[:, u, :], start=True, stop=True)\
                                    .then_inc(s_qk, 1)
                            pe.wait_ge(s_vp, 2 * b + BASE)
                            for t in range(CT):
                                mm = nc.tensor.matmul(ps[:, 6 + u, t * P:(t + 1) * P], xnT[:, u, t * P:(t + 1) * P],
                                                      wv, start=True, stop=True)
                            mm.then_inc(s_v, 1)

                @block.scalar
                def _(act):
                    with act.Fori(0, BATCH) as b:
                        for u in range(2):
                            act.wait_ge(s_T, 2 * b + u + 1 + BASE)
                            act.wait_ge(s_v, 2 * b + BASE)
                            nc.scalar.activation(xnT[:, u, :], ps[:, u, :], ACT.Copy).then_inc(s_xT, 1)
                        for u in range(2):
                            act.wait_ge(s_st[u], 16 * 7 * b + BASE)
                            for s in range(2):
                                act.wait_ge(s_qk, 4 * b + 2 * u + s + 1 + BASE)
                                nc.scalar.activation(parts[:, u, s, 0, :], ps[:, 2 + 2 * s + u, :], ACT.Copy)\
                                    .then_inc(s_p1, 1)
                            for s in range(2):
                                act.wait_ge(s_r1, 4 * b + 2 * u + s + 1 + BASE)
                                nc.scalar.activation(parts[:, u, s, 1, :], rest[:, u, s, :], ACT.Copy)\
                                    .then_inc(s_p2, 1)

                @block.sync
                def _(sp):
                    sp.wait_ge(s_pad, 2 + BASE)
                    with sp.Fori(0, BATCH) as b:
                        for u in range(2):
                            sp.wait_ge(s_vp, 2 * b + u + 1 + BASE)
                            sp.dma_start(
                                v8_d[bass.ds(b * T + u * CH, CH), :].rearrange("(t p) w -> p t w", p=P),
                                v_pad[:, u, :, :, :].rearrange("p t h w -> p t (h w)")).then_inc(s_st[u], 16)
                            sp.wait_ge(s_p3, 4 * b + 2 * u + 2 + BASE)
                            for s, d in enumerate((q8_d, k8_d)):
                                for part in range(3):
                                    sp.dma_start(
                                        d[bass.ds(b * NQ, NQ), :, part, :, :, u * CH:(u + 1) * CH]
                                        .rearrange("n a d h t -> n a (d h) t"),
                                        parts[:, u, s, part, :]).then_inc(s_st[u], 16)
                    for u in range(2):
                        sp.wait_ge(s_st[u], 16 * 7 * BATCH + BASE)

        def attention(name, scale, latent, has_max, clip):
            S_BANKS, M_BANKS = (4, 2) if has_max else (6, 0)
            LEAD = 12
            o_bank, s_bank0, m_bank0 = 0, 2, 6
            PRING = 3
            n_loads = (6 + 3 + 1) if latent else (2 * (6 + 3 + has_max) + 1)
            qs = q_buf[:, :, :].rearrange("p n (c h t) -> p n c h t", c=3, h=QUAD)
            ks = k_buf[:, :, :].rearrange("p n (c t) -> p n c t", c=3)
            if latent:
                vs = v_buf[:, :, 0:KB * VW].rearrange("p n (k w) -> p n k w", k=KB)
            else:
                vs = v_buf[:, :, :].rearrange("p n (k w) -> p n k w", k=KB)
            nm = name
            s_ld = [sem(f"{nm}_ld{s}") for s in range(NB)]
            s_mrow = [sem(f"{nm}_mrow{s}") for s in range(NB)]
            s_s = sem(nm + "_s")
            s_e = sem(nm + "_e")
            s_clip = sem(nm + "_clip")
            s_sel = sem(nm + "_sel")
            s_pv = sem(nm + "_pv")
            s_oc = sem(nm + "_oc")
            s_ost = sem(nm + "_ost")
            s_m = sem(nm + "_m")
            s_mr = sem(nm + "_mr")
            s_pm = sem(nm + "_pm")
            s_mT = sem(nm + "_mT")
            s_m1 = sem(nm + "_m1")
            s_m2 = sem(nm + "_m2")
            s_m3 = sem(nm + "_m3")
            s_m4 = sem(nm + "_m4")
            s_mst = sem(nm + "_mst")
            s_one = sem(nm + "_one")
            s_oneld = [sem(nm + f"_oneld{h}") for h in range(2)]
            s_pi = sem(nm + "_pi")
            s_clear = [sem(nm + f"_clear{e}") for e in range(2)]

            def clear(eng, slots, done):
                for s in slots:
                    eng.memset(q_buf[:, s, 0:6 * T].bitcast(F32), 0.0).then_inc(done, 1)
            minus_one = o_sb[0:3, 0, :].bitcast(BF16)

            diag = [[s for s in unit if s[0] == s[1]] for unit in S_UNITS]
            diags_before = [sum(QUAD * len(d) for d in diag[:g]) for g in range(ROWS_P + 1)]
            DIAGS = diags_before[-1]

            def m_events(n, t, last):
                k = t + LEAD
                off, k = 1 + k // UNITS, k % UNITS
                if last is not None and last + off >= ITEMS:
                    return []
                return [(off, k)]

            def slot(i, off=0):
                return (i + off) % NB

            def uses(b, i, off=0):
                return b + (i + off) // NB + 1

            def run_items(eng, item, first=None, rest=None):
                if first is not None:
                    first()
                item(0, 0, 0)
                with eng.Fori(0, BATCH - 1) as b:
                    for i in range(1, NQ + 1):
                        item(b, i, None)
                for i in range(1, NQ):
                    item(BATCH - 1, i, (BATCH - 1) * NQ + i)
                if rest is not None:
                    rest()

            def count_of(eng, b, i):
                if isinstance(b, int):
                    return b * NQ + i
                count = eng.alloc_register()
                eng.reg_mov(count, b * NQ + i)
                return eng.snap(count, donate=True, min_val=i, max_val=(BATCH - 2) * NQ + i)

            with nc.Block() as block:
                @block.sync
                def _(sp):
                    def load(b, i, off):
                        s = slot(i, off)
                        n = b * NQ + i + off
                        if latent:
                            for c in range(3):
                                for hf in range(2):
                                    t = 2 * c + hf
                                    sp.dma_start(qs[48 * hf:48 * hf + MD, s, c, :, :],
                                                 qm_d[bass.ds(n, 1), QTERM[t], :, :, :]
                                                 .rearrange("n r h t -> (n r) h t")).then_inc(s_ld[s], 16)
                            seq = b + (i + off) // NQ
                            for c in range(3):
                                sp.dma_start(ks[0:2 * MD, s, c, :],
                                             kterm_d[c][bass.ds(seq, 1), :, :]
                                             .rearrange("n r t -> (n r) t")).then_inc(s_ld[s], 16)
                            sp.dma_start(vs[:, s, :, :],
                                         vm_d[bass.ds(seq * T, T), :].rearrange("(k p) w -> p k w", p=P))\
                                .then_inc(s_ld[s], 16)
                        else:
                            seq = b + (i + off) // NQ
                            quad = (i + off) % NQ
                            for pr in range(2):
                                for t in range(6):
                                    sp.dma_start(qs[64 * pr + 8 * t:64 * pr + 8 * t + 8, s, 0, pr:QUAD:2, :],
                                                 q8_d[bass.ds(n, 1), pr, QTERM[t], :, :, :]
                                                 .rearrange("n d h t -> (n d) h t")).then_inc(s_ld[s], 16)
                                for t0, cnt in ((0, 3), (3, 2), (5, 1)):
                                    sp.dma_start(
                                        qs[64 * pr + 8 * t0:64 * pr + 8 * (t0 + cnt), s, 1, 0:2, :],
                                        k8_d[bass.ds(n, 1), pr, 0:cnt, :, :, :]
                                        .rearrange("n c d h t -> (n c d) h t")).then_inc(s_ld[s], 16)
                            if has_max:
                                for pr in range(2):
                                    sp.dma_start(qs[64 * pr + 48:64 * pr + 51, s, 0, pr:QUAD:2, :],
                                                 qs[51:54, s, 0, pr:QUAD:2, :])\
                                        .then_inc(s_ld[s], 16)
                            sp.dma_start(vs[:, s, :, :],
                                         v8_d[bass.ds(seq * T, T), quad * QUAD * VW:(quad + 1) * QUAD * VW]
                                         .rearrange("(k p) w -> p k w", p=P)).then_inc(s_ld[s], 16)

                    def maxima(b, i, off):
                        n = b * NQ + i + off
                        s = slot(i, off)
                        sp.wait_ge(s_m4, n + 1 + BASE)
                        for a in range(P // MR):
                            sp.dma_start(mx_d[bass.ds(n, 1), :, :, :]
                                         .rearrange("n c h (k a q) -> a (n h k) c q", a=P // MR, q=MR)[a],
                                         m_parts[MR * a:MR * (a + 1), (i + off) % 2, :, :]).then_inc(s_mst, 16)
                        sp.wait_ge(s_mst, 16 * (P // MR) * (n + 1) + BASE)
                        if latent:
                            for c in range(3):
                                sp.dma_start(qs[96:97, s, c, :, :], mx_d[bass.ds(n, 1), c, :, :])\
                                    .then_inc(s_mrow[s], 16)
                        else:
                            for pr in range(2):
                                sp.dma_start(qs[64 * pr + 48:64 * pr + 51, s, 0, pr:QUAD:2, :],
                                             mx_d[bass.ds(n, 1), :, :, :]
                                             .rearrange("n c (a r) t -> (n c) a r t", r=2)[:, :, pr, :])\
                                    .then_inc(s_mrow[s], 16)

                    def take_off_rows(half):
                        for s in (2 * half, 2 * half + 1):
                            for pr in range(2):
                                sp.dma_start(qs[64 * pr + 48:64 * pr + 51, s, 1, 0:2, :],
                                             minus_one.rearrange("p (a t) -> p a t", a=2))\
                                    .then_inc(s_oneld[half], 16)

                    def first():
                        if not latent:
                            sp.wait_ge(s_clear[0], 2 + BASE)
                        load(0, 0, 0)
                        load(0, 0, 1)
                        if has_max and not latent:
                            sp.wait_ge(s_one, 1 + BASE)
                            take_off_rows(0)
                        if not latent:
                            sp.wait_ge(s_clear[1], 2 + BASE)
                        if has_max and not latent:
                            take_off_rows(1)
                        if has_max:
                            maxima(0, 0, 0)

                    def item(b, i, last):
                        n = b * NQ + i
                        if last is None or last + 2 < ITEMS:
                            sp.wait_ge(s_s, UNITS * n + BASE)
                            load(b, i, 2)
                        if last != 0:
                            store(n - 1)
                        if has_max and (last is None or last + 1 < ITEMS):
                            maxima(b, i, 1)

                    def store(n):
                        sp.wait_ge(s_oc, n + 1 + BASE)
                        sp.dma_start(o_d[bass.ds(n, 1), :, :].rearrange("n p t -> (n p) t"), o_sb[:, 0, :])\
                            .then_inc(s_ost, 16)

                    run_items(sp, item, first, lambda: store(ITEMS - 1))
                    sp.wait_ge(s_ost, 16 * ITEMS + BASE)

                @block.tensor
                def _(pe):
                    def score_unit(n, i, t):
                        g, j = divmod(t, QUAD)
                        bank = s_bank0 + t % S_BANKS
                        s = slot(i)
                        pe.wait_ge(s_e, UNITS * n + t + 1 + BASE)
                        for k, q0, nq, off in S_UNITS[g]:
                            o = ps[:, bank, off * P:(off + nq) * P]
                            if latent:
                                for c in range(3):
                                    mm = nc.tensor.matmul(o, ks[0:97, s, c, k * P:(k + 1) * P],
                                                          qs[0:97, s, c, j, q0 * P:(q0 + nq) * P],
                                                          start=(c == 0), stop=(c == 2))
                            else:
                                mm = nc.tensor.matmul(o, qs[:, s, 1, j // 2, k * P:(k + 1) * P],
                                                      qs[:, s, 0, j, q0 * P:(q0 + nq) * P],
                                                      start=True, stop=True)
                        mm.then_inc(s_s, 1)

                    def max_unit(m, b, i, off, k):
                        j, g = divmod(k, ROWS_P)
                        n = m + off
                        s = slot(i, off)
                        if k == 0:
                            pe.wait_ge(s_ld[s], 16 * n_loads * uses(b, i, off) + BASE)
                        pe.wait_ge(s_mr, UNITS * n + k + 1 + BASE)
                        bank = m_bank0 + k % M_BANKS
                        for q, k0, nk, o_, _ in M_UNITS[g]:
                            o = ps[:, bank, o_ * P:(o_ + nk) * P]
                            has_diag = k0 + nk - 1 == q
                            if latent:
                                mm = nc.tensor.matmul(o, qs[0:96, s, 0, j, q * P:(q + 1) * P],
                                                      ks[0:96, s, 0, k0 * P:(k0 + nk) * P],
                                                      start=True, stop=not has_diag, skip_group_check=True)
                            else:
                                mm = nc.tensor.matmul(o, qs[:, s, 0, j, q * P:(q + 1) * P],
                                                      qs[:, s, 1, j // 2, k0 * P:(k0 + nk) * P],
                                                      start=True, stop=not has_diag, skip_group_check=True)
                            if has_diag:
                                mm = nc.tensor.matmul(ps[:, bank, (o_ + nk - 1) * P:(o_ + nk) * P],
                                                      ident_bf[:, :], causal_bf[:, :], start=False, stop=True,
                                                      skip_group_check=True)
                        mm.then_inc(s_m, 1)

                    def value_row(n, i, g):
                        s = slot(i)
                        pe.wait_ge(s_e, UNITS * n + QUAD * (g + 1) + S_BANKS + BASE)
                        if clip:
                            pe.wait_ge(s_clip, UNITS * n + QUAD * (g + 1) + BASE)
                        pe.wait_ge(s_sel, DIAGS * n + diags_before[g + 1] + BASE)
                        if g == 0:
                            pe.wait_ge(s_oc, n + BASE)
                        for k, q0, nq, off in S_UNITS[g]:
                            for bank, lo, hi in ((0, 0, 4), (1, 4, 8)):
                                a, z = max(q0, lo), min(q0 + nq, hi)
                                if a >= z:
                                    continue
                                for j in range(QUAD):
                                    v = vs[:, s, k, 0:VW] if latent else vs[:, s, k, j * VW:(j + 1) * VW]
                                    mm = nc.tensor.matmul(
                                        ps[VW * j:VW * (j + 1), o_bank + bank, (a - lo) * P:(z - lo) * P], v,
                                        pr_buf[:, (g % PRING) * QUAD + j, (off + a - q0) * P:(off + z - q0) * P],
                                        start=(k == 0), stop=(k == hi - 1), tile_position=(0, VW * j),
                                        skip_group_check=True)
                        mm.then_inc(s_pv, 1)

                    def first():
                        pe.sem_inc(s_pv, PRING)
                        if has_max:
                            if not latent:
                                pe.wait_ge(s_oneld[0], 16 * 4 + BASE)
                            for k in range(UNITS):
                                max_unit(0, 0, 0, 0, k)
                            for k in range(LEAD):
                                max_unit(0, 0, 0, 1, k)
                            if not latent:
                                pe.wait_ge(s_oneld[1], 16 * 4 + BASE)
                            else:
                                pe.wait_ge(s_one, 1 + BASE)

                    def item(b, i, last):
                        s = slot(i)
                        n = count_of(pe, b, i)
                        if has_max:
                            pe.wait_ge(s_mrow[s], 16 * (3 if latent else 2) * uses(b, i) + BASE)
                        pe.wait_ge(s_ld[s], 16 * n_loads * uses(b, i) + BASE)
                        for t in range(UNITS):
                            score_unit(n, i, t)
                            if has_max:
                                for off, k in m_events(None, t, last):
                                    max_unit(n, b, i, off, k)
                            if t == QUAD - 1 and last != 0:
                                value_row(n - 1, i - 1, ROWS_P - 1)
                            if t % QUAD == QUAD - 1 and t >= QUAD:
                                value_row(n, i, t // QUAD - 1)

                    run_items(pe, item, first, lambda: value_row(ITEMS - 1, ITEMS - 1, ROWS_P - 1))

                @block.scalar
                def _(act):
                    def item(b, i, last):
                        n = b * NQ + i
                        for t in range(UNITS):
                            g, j = divmod(t, QUAD)
                            act.wait_ge(s_s, UNITS * n + t + 1 + BASE)
                            if j == 0:
                                act.wait_ge(s_pv, ROWS_P * n + g + 1 + BASE)
                            nc.scalar.activation(pr_buf[:, (g % PRING) * QUAD + j, :],
                                                 ps[:, s_bank0 + t % S_BANKS, :], ACT.Exp, scale=scale)\
                                .then_inc(s_e, 1)

                    run_items(act, item, lambda: act.sem_inc(s_e, S_BANKS))

                @block.gpsimd
                def _(pool):
                    def item(b, i, last):
                        n = b * NQ + i
                        for t in range(UNITS):
                            g, j = divmod(t, QUAD)
                            for k, q0, nq, off in diag[g]:
                                if clip:
                                    wait_alone(pool, s_clip, UNITS * n + t + 1)
                                else:
                                    wait_alone(pool, s_e, UNITS * n + t + 1 + S_BANKS)
                                blk = pr_buf[:, (g % PRING) * QUAD + j, off * P:(off + 1) * P]
                                nc.gpsimd.affine_select(out=blk, in_=blk, compare_op=ALU.is_ge, fill=0.0, base=0,
                                                        pattern=[[1, P]], channel_multiplier=-1).then_inc(s_sel, 1)

                    if has_max and not latent:
                        nc.gpsimd.memset(minus_one, -1.0).then_inc(s_one, 1)
                    if not latent:
                        clear(pool, (2, 3), s_clear[1])
                    run_items(pool, item)

                @block.vector
                def _(dve):
                    def reduce_unit(m, i, off, k):
                        j, g = divmod(k, ROWS_P)
                        n = m + off
                        dve.wait_ge(s_m, UNITS * n + k + 1 + BASE)
                        if k == 0:
                            dve.wait_ge(s_pm, n + BASE)
                        bank = m_bank0 + k % M_BANKS
                        for q, k0, nk, o_, part in M_UNITS[g]:
                            r = nc.vector.tensor_reduce(pmax[:, j, q, part:part + 1],
                                                        ps[:, bank, o_ * P:(o_ + nk) * P], AX_X, ALU.max)
                        r.then_inc(s_mr, 1)
                        if k == UNITS - 1:
                            dve.wait_ge(s_mr, UNITS * (n + 1) + M_BANKS + BASE)
                            if not (isinstance(n, int) and n == 0):
                                dve.wait_ge(s_mT, n + BASE)
                            nc.vector.tensor_reduce(mx_sb[:, (i + off) % 2, :],
                                                    pmax[:, :, :, :].rearrange("p j q a -> p (j q) a"),
                                                    AX_X, ALU.max).then_inc(s_pm, 1)

                    def split_maxima(m, i, off):
                        n = m + off
                        mp = m_parts[:, (i + off) % 2, :, :]
                        dve.wait_ge(s_pm, n + 1 + BASE)
                        dve.wait_ge(s_m4, n + BASE)
                        nc.vector.transpose(mx_turned[:, :], mx_sb[:, (i + off) % 2, :]).then_inc(s_mT, 1)
                        dve.wait_ge(s_mT, n + 1 + BASE)
                        dve.wait_ge(s_mst, 16 * (P // MR) * n + BASE)
                        nc.vector.tensor_copy(mp[:, 0, :], mx_turned[:, :]).then_inc(s_m1, 1)
                        dve.wait_ge(s_m1, n + 1 + BASE)
                        nc.vector.tensor_tensor(m_rest[:, :], mx_turned[:, :], mp[:, 0, :], ALU.subtract)\
                            .then_inc(s_m2, 1)
                        dve.wait_ge(s_m2, n + 1 + BASE)
                        nc.vector.tensor_copy(mp[:, 1, :], m_rest[:, :]).then_inc(s_m3, 1)
                        dve.wait_ge(s_m3, n + 1 + BASE)
                        nc.vector.tensor_tensor(mp[:, 2, :], m_rest[:, :], mp[:, 1, :], ALU.subtract)\
                            .then_inc(s_m4, 1)

                    def first():
                        if not latent:
                            clear(dve, (0, 1), s_clear[0])
                        if has_max:
                            dve.sem_inc(s_mr, M_BANKS)
                            nc.vector.memset(pmax[:, :, :, :], -3.0e38).then_inc(s_pi, 1)
                            if latent:
                                nc.vector.memset(ks[96:97, :, :, :], -1.0).then_inc(s_one, 1)
                            dve.wait_ge(s_pi, 1 + BASE)
                            for k in range(UNITS):
                                reduce_unit(0, 0, 0, k)
                            split_maxima(0, 0, 0)
                            for k in range(LEAD):
                                reduce_unit(0, 0, 1, k)

                    def copy_outputs(n):
                        dve.wait_ge(s_pv, ROWS_P * (n + 1) + PRING + BASE)
                        dve.wait_ge(s_ost, 16 * n + BASE)
                        nc.vector.tensor_copy(o_sb[:, 0, :].rearrange("p (a t) -> p a t", a=2),
                                              ps[:, o_bank:o_bank + 2, :]).then_inc(s_oc, 1)

                    def item(b, i, last):
                        n = count_of(dve, b, i)
                        for t in range(UNITS):
                            g, j = divmod(t, QUAD)
                            if clip:
                                dve.wait_ge(s_e, UNITS * n + t + 1 + S_BANKS + BASE)
                                p = pr_buf[:, (g % PRING) * QUAD + j, :]
                                nc.vector.tensor_scalar(p, p, float(np.exp(-10.0)), float(np.exp(10.0)),
                                                        ALU.max, ALU.min).then_inc(s_clip, 1)
                            if has_max:
                                for off, k in m_events(None, t, last):
                                    reduce_unit(n, i, off, k)
                                if t == UNITS - LEAD + 1 and (last is None or last + 1 < ITEMS):
                                    split_maxima(n, i, 1)
                            if t == QUAD - 1 and last != 0:
                                copy_outputs(n - 1)

                    run_items(dve, item, first, lambda: copy_outputs(ITEMS - 1))

        def finish_heads8(name, wo):
            area_at[0] = 0
            norm = Norm(name + "ln")
            oT = work(2, NQ, CH)
            rden = work(2, CT, HEADS)
            on = work(2, CT, C)
            onT = work(2, CH)
            y = work(2, CT, C)
            s_ld = [sem(f"{name}_ld{u}") for u in range(2)]
            s_T = sem(name + "_T")
            s_rd = sem(name + "_rd")
            s_on = sem(name + "_on")
            s_T2 = sem(name + "_T2")
            s_c2 = sem(name + "_c2")
            s_y = sem(name + "_y")
            s_yc = sem(name + "_yc")
            s_res = sem(name + "_res")
            s_nr = sem(name + "_nr")
            with nc.Block() as block:
                @block.sync
                def _(sp):
                    with sp.Fori(0, BATCH) as b:
                        for u in range(2):
                            sp.wait_ge(s_T, 4 * 2 * b + BASE)
                            sp.dma_start(oT[:, u, :, :],
                                         o_d[bass.ds(b * NQ, NQ), :, u * CH:(u + 1) * CH]
                                         .rearrange("n p t -> p n t")).then_inc(s_ld[u], 16)

                @block.tensor
                def _(pe):
                    pe.sem_inc(s_rd, 0) if False else None
                    with pe.Fori(0, BATCH) as b:
                        for u in range(2):
                            pe.wait_ge(s_ld[u], 16 * (b + 1) + BASE)
                            for t in range(CT):
                                pe.wait_ge(s_on, 8 * b + 4 * u + t + 1 + BASE)
                                for q in range(NQ):
                                    i = nc.tensor.transpose(ps[:, t % 2, q * P:(q + 1) * P],
                                                            oT[:, u, q, t * P:(t + 1) * P], identity[:, :])
                                i.then_inc(s_T, 1)
                        if wo is not None:
                            for u in range(2):
                                pe.wait_ge(s_on, 8 * b + 4 * u + 4 + 2 + BASE)
                                pe.wait_ge(s_c2, 2 * b + BASE)
                                transpose_chunk(2 + u, on[:, u, :, :]).then_inc(s_T2, 1)
                            for u in range(2):
                                pe.wait_ge(s_c2, 2 * b + u + 1 + BASE)
                                pe.wait_ge(s_yc, 2 * b + BASE)
                                for t in range(CT):
                                    i = nc.tensor.matmul(ps[:, 4 + u, t * P:(t + 1) * P],
                                                         onT[:, u, t * P:(t + 1) * P], wo, start=True, stop=True)
                                i.then_inc(s_y, 1)

                @block.scalar
                def _(act):
                    if wo is not None:
                        with act.Fori(0, BATCH) as b:
                            for u in range(2):
                                act.wait_ge(s_T2, 2 * b + u + 1 + BASE)
                                act.wait_ge(s_y, 2 * b + BASE)
                                nc.scalar.activation(onT[:, u, :], ps[:, 2 + u, :], ACT.Copy).then_inc(s_c2, 1)
                            for u in range(2):
                                act.wait_ge(s_y, 2 * b + u + 1 + BASE)
                                act.wait_ge(s_res, 2 * b + BASE)
                                nc.scalar.activation(y[:, u, :, :].rearrange("p a b -> p (a b)"), ps[:, 4 + u, :],
                                                     ACT.Copy).then_inc(s_yc, 1)

                @block.gpsimd
                def _(pool):
                    with pool.Fori(0, BATCH) as b:
                        for u in range(2):
                            norm.inverse(pool, b, u)

                @block.vector
                def _(dve):
                    dve.sem_inc(s_on, 2)
                    with dve.Fori(0, BATCH) as b:
                        for u in range(2):
                            if wo is not None:
                                dve.wait_ge(s_T2, 2 * b + BASE)
                            else:
                                dve.wait_ge(norm.s_out, 2 * b + BASE)
                            for t in range(CT):
                                dve.wait_ge(s_T, 8 * b + 4 * u + t + 1 + BASE)
                                o3 = ps[:, t % 2, :].rearrange("p (h w) -> p h w", w=VW)
                                nc.vector.reciprocal(rden[:, u, t, :], o3[:, :, 8]).then_inc(s_rd, 1)
                                dve.wait_ge(s_rd, 8 * b + 4 * u + t + 1 + BASE)
                                nc.vector.tensor_tensor(
                                    on[:, u, t, :].rearrange("p (h d) -> p h d", d=8), o3[:, :, 0:8],
                                    rden[:, u, t, :].unsqueeze(2).to_broadcast([P, HEADS, 8]), ALU.mult)\
                                    .then_inc(s_on, 1)
                        for u in range(2):
                            if wo is not None:
                                dve.wait_ge(s_yc, 2 * b + u + 1 + BASE)
                            else:
                                dve.wait_ge(s_on, 8 * b + 4 * u + 4 + 2 + BASE)
                            norm.stats(dve, b, u, (y if wo is not None else on)[:, u, :, :])
                        for u in range(2):
                            src = (y if wo is not None else on)[:, u, :, :]
                            norm.apply(dve, b, u, src, src)
                            dve.wait_ge(norm.s_out, 2 * b + u + 1 + BASE)
                            nc.vector.tensor_tensor(tiles_of(x_res, b, u), tiles_of(x_res, b, u), src, ALU.add)\
                                .then_inc(s_res, 1)

        def project_latent():
            name = "pl"
            area_at[0] = 0
            norm = Norm(name + "ln")
            rms = RootMean(name + "rm")
            xr = work(2, CT, C)
            xrT = work(2, CH)
            JOBS = 7
            t_cos = work(2, CH)
            t_sin = work(2, CH)
            val = work(2, CH)
            rest = work(2, CH)
            parts = work(4, 3, CH, dt=BF16)
            v_pad = work(2, CT, VW)
            xx = work(2, CT, C)
            table = {n: work(T, parts=consts[n].shape[0]) for n in TABLES}
            s_tab = sem(name + "_tab")
            s_xst = [sem(f"{name}_xst{u}") for u in range(2)]
            s_pad = sem(name + "_pad")
            s_T = sem(name + "_T")
            s_xT = sem(name + "_xT")
            s_v = sem(name + "_v")
            s_vp = sem(name + "_vp")
            s_vst = [sem(f"{name}_vst{u}") for u in range(2)]
            s_mm = sem(name + "_mm")
            s_cs = sem(name + "_cs")
            s_val = sem(name + "_val")
            s_p1 = sem(name + "_p1")
            s_r1 = sem(name + "_r1")
            s_p2 = sem(name + "_p2")
            s_p3 = sem(name + "_p3")
            s_st = [sem(f"{name}_st{s}") for s in range(4)]
            tab = {True: ("cos_k", "sin_k"), False: ("cos_q", "sin_q")}

            def job(b, u, j):
                return b * 2 * JOBS + u * JOBS + j, (u * JOBS + j) % 2, (MD if j == 6 else P), j not in (4, 5)

            def slot4(u, j):
                return (u * JOBS + j) % 4

            def n_dma(j):
                return 6 if j == 6 else 3

            seq_total = [sum(n_dma(j) for u in range(2) for j in range(JOBS) if slot4(u, j) == s) for s in range(4)]

            def before(u, j):
                s = slot4(u, j)
                return sum(n_dma(jj) for uu in range(2) for jj in range(JOBS)
                           if slot4(uu, jj) == s and (uu, jj) < (u, j))

            def third_part(dve, b, u, j):
                n, r, rows, rot = job(b, u, j)
                dve.wait_ge(s_p2, n + 1 + BASE)
                s = slot4(u, j)
                nc.vector.tensor_tensor(parts[0:rows, s, 2, :], rest[0:rows, r, :], parts[0:rows, s, 1, :],
                                        ALU.subtract).then_inc(s_p3, 1)

            with nc.Block() as block:
                @block.vector
                def _(dve):
                    nc.vector.memset(v_pad, 0.0).then_inc(s_pad, 1)
                    dve.wait_ge(s_pad, 1 + BASE)
                    nc.vector.memset(v_pad[:, :, :, LAT:LAT + 1], 1.0).then_inc(s_pad, 1)
                    dve.sem_inc(s_cs, 2)
                    dve.wait_ge(s_tab, 16 * len(TABLES) + BASE)
                    with dve.Fori(0, BATCH) as b:
                        for u in range(2):
                            norm.stats(dve, b, u, tiles_of(x_res, b, u))
                        for u in range(2):
                            dve.wait_ge(rms.s_out, 2 * b + BASE)
                            dve.wait_ge(s_xst[u], 16 * b + BASE)
                            norm.apply(dve, b, u, tiles_of(x_res, b, u), xx[:, u, :, :])
                        for u in range(2):
                            dve.wait_ge(s_v, 2 * b + u + 1 + BASE)
                            dve.wait_ge(s_vst[u], 16 * b + BASE)
                            nc.vector.tensor_copy(v_pad[:, u, :, 0:LAT],
                                                  ps[:, 2 + u, 0:CT * LAT].rearrange("p (t r) -> p t r", t=CT))\
                                .then_inc(s_vp, 1)
                            for j in range(JOBS):
                                n, r, rows, rot = job(b, u, j)
                                dve.wait_ge(s_mm, n + 1 + BASE)
                                dve.wait_ge(s_val, n + BASE)
                                if rot:
                                    cs, sn = tab[j == 6]
                                    nc.vector.tensor_tensor(t_cos[0:rows, r, :], ps[0:rows, 4 + 2 * r, :],
                                                            table[cs][:, u * CH:(u + 1) * CH], ALU.mult)
                                    nc.vector.tensor_tensor(t_sin[0:rows, r, :], ps[0:rows, 5 + 2 * r, :],
                                                            table[sn][:, u * CH:(u + 1) * CH], ALU.mult)\
                                        .then_inc(s_cs, 1)
                                else:
                                    nc.vector.tensor_copy(t_cos[:, r, :], ps[:, 4 + 2 * r, :])\
                                        .then_inc(s_cs, 1)
                                if j >= 1:
                                    third_part(dve, b, u, j - 1)
                            third_part(dve, b, u, JOBS - 1)

                @block.gpsimd
                def _(pool):
                    pool.sem_inc(rms.s_go, 1)
                    with pool.Fori(0, BATCH) as b:
                        for u in range(2):
                            norm.inverse(pool, b, u)
                        for u in range(2):
                            rms.inverse(pool, b, u)
                        for u in range(2):
                            for j in range(JOBS):
                                n, r, rows, rot = job(b, u, j)
                                pool.wait_ge(s_r1, n + BASE)
                                wait_alone(pool, s_cs, n + 1 + 2)
                                if rot:
                                    nc.gpsimd.tensor_tensor(val[0:rows, r, :], t_cos[0:rows, r, :],
                                                            t_sin[0:rows, r, :], ALU.add).then_inc(s_val, 1)
                                else:
                                    nc.gpsimd.tensor_copy(val[:, r, :], t_cos[:, r, :]).then_inc(s_val, 1)
                                pool.wait_ge(s_p1, n + 1 + BASE)
                                pool.wait_ge(s_p3, n + 1 + BASE)
                                nc.gpsimd.tensor_tensor(rest[0:rows, r, :], val[0:rows, r, :],
                                                        parts[0:rows, slot4(u, j), 0, :], ALU.subtract)\
                                    .then_inc(s_r1, 1)

                @block.tensor
                def _(pe):
                    with pe.Fori(0, BATCH) as b:
                        for u in range(2):
                            pe.wait_ge(rms.s_out, 2 * b + u + 1 + BASE)
                            pe.wait_ge(s_xT, 2 * b + BASE)
                            transpose_chunk(u, xr[:, u, :, :]).then_inc(s_T, 1)
                        for u in range(2):
                            pe.wait_ge(s_xT, 2 * b + u + 1 + BASE)
                            pe.wait_ge(s_vp, 2 * b + BASE)
                            for t in range(CT):
                                i = nc.tensor.matmul(ps[:, 2 + u, t * LAT:(t + 1) * LAT],
                                                     xrT[:, u, t * P:(t + 1) * P], w_sb["wkva"][:, 0:LAT],
                                                     start=True, stop=True)
                            i.then_inc(s_v, 1)
                            for j in range(JOBS):
                                n, r, rows, rot = job(b, u, j)
                                pe.wait_ge(s_cs, n + 1 + BASE)
                                if j < 4:
                                    wa, wb = w_sb["wq_rope"][:, j, :], w_sb["wq_rope_sw"][:, j, :]
                                elif j < 6:
                                    wa = wabs[:, j - 4, :, :, :].rearrange("p a b c -> p (a b c)")
                                else:
                                    wa, wb = w_sb["wkva"][:, :], w_sb["wkva_sw"][:, :]
                                i = nc.tensor.matmul(ps[0:rows, 4 + 2 * r, :], wa, xrT[:, u, :], start=True, stop=True)
                                if rot:
                                    i = nc.tensor.matmul(ps[0:rows, 5 + 2 * r, :], wb, xrT[:, u, :],
                                                         start=True, stop=True)
                                i.then_inc(s_mm, 1)

                @block.scalar
                def _(act):
                    with act.Fori(0, BATCH) as b:
                        for u in range(2):
                            act.wait_ge(norm.s_out, 2 * b + u + 1 + BASE)
                            rms.squares(act, b, u, xx[:, u, :, :])
                        for u in range(2):
                            rms.apply(act, b, u, xx[:, u, :, :], xr[:, u, :, :], (s_T, 2 * b))
                        for u in range(2):
                            act.wait_ge(s_T, 2 * b + u + 1 + BASE)
                            act.wait_ge(s_mm, 2 * JOBS * b + BASE)
                            nc.scalar.activation(xrT[:, u, :], ps[:, u, :], ACT.Copy, scale=w_sb["ln1"][:, 0:1])\
                                .then_inc(s_xT, 1)
                        for u in range(2):
                            for j in range(JOBS):
                                n, r, rows, rot = job(b, u, j)
                                s = slot4(u, j)
                                act.wait_ge(s_val, n + 1 + BASE)
                                act.wait_ge(s_st[s], 16 * (seq_total[s] * b + before(u, j)) + BASE)
                                nc.scalar.activation(parts[0:rows, s, 0, :], val[0:rows, r, :], ACT.Copy)\
                                    .then_inc(s_p1, 1)
                                act.wait_ge(s_r1, n + 1 + BASE)
                                nc.scalar.activation(parts[0:rows, s, 1, :], rest[0:rows, r, :], ACT.Copy)\
                                    .then_inc(s_p2, 1)

                @block.sync
                def _(sp):
                    sp.wait_ge(s_pad, 2 + BASE)
                    sp.sem_inc(s_p3, 2)
                    for n in TABLES:
                        sp.dma_start(table[n], consts[n]).then_inc(s_tab, 16)
                    with sp.Fori(0, BATCH) as b:
                        for u in range(2):
                            sp.wait_ge(norm.s_out, 2 * b + u + 1 + BASE)
                            sp.dma_start(xx_d[bass.ds(b * T + u * CH, CH), :].rearrange("(t p) c -> p t c", p=P),
                                         xx[:, u, :, :]).then_inc(s_xst[u], 16)
                        for u in range(2):
                            sp.wait_ge(s_vp, 2 * b + u + 1 + BASE)
                            sp.dma_start(vm_d[bass.ds(b * T + u * CH, CH), :].rearrange("(t p) w -> p t w", p=P),
                                         v_pad[:, u, :, :]).then_inc(s_vst[u], 16)
                            tok = slice(u * CH, (u + 1) * CH)
                            for j in range(JOBS):
                                n, r, rows, rot = job(b, u, j)
                                s = slot4(u, j)
                                wait_alone(sp, s_p3, n + 1 + 2)
                                if j < 4:
                                    for part in range(3):
                                        sp.dma_start(qm_d[bass.ds(b * NQ + j, 1), part, LAT:MD, :, tok]
                                                     .rearrange("n r h t -> (n r h) t"),
                                                     parts[:, s, part, :]).then_inc(s_st[s], 16)
                                elif j < 6:
                                    for part in range(3):
                                        sp.dma_start(qm_d[bass.ds(b * NQ + 2 * (j - 4), 2), part, 0:LAT, :, tok]
                                                     .rearrange("n r h t -> n (r h) t"),
                                                     parts[:, s, part, :]).then_inc(s_st[s], 16)
                                else:
                                    for t in range(6):
                                        sp.dma_start(kterm_d[t // 2][bass.ds(b, 1), (t % 2) * MD:(t % 2 + 1) * MD, tok]
                                                     .rearrange("n r t -> (n r) t"),
                                                     parts[0:MD, s, KTERM[t], :]).then_inc(s_st[s], 16)
                    for u in range(2):
                        sp.wait_ge(s_vst[u], 16 * BATCH + BASE)
                        sp.wait_ge(s_xst[u], 16 * BATCH + BASE)
                    for s in range(4):
                        sp.wait_ge(s_st[s], 16 * seq_total[s] * BATCH + BASE)

        x2_res = v_buf[:, :, :].rearrange("p a b -> p (a b)").rearrange("p (t c) -> p t c", c=C)

        def finish_latent():
            name = "fl"
            area_at[0] = 0
            oT = work(2, NQ, CH)
            rden = work(2, CT, HEADS)
            on = work(2, CT, 2 * P)
            onT = work(2, 2, CH)
            xx = work(2, CT, C)
            s_xx = [sem(f"{name}_xx{u}") for u in range(2)]
            s_ld = [sem(f"{name}_ld{u}") for u in range(2)]
            s_T = sem(name + "_T")
            s_rd = sem(name + "_rd")
            s_on = sem(name + "_on")
            s_T2 = sem(name + "_T2")
            s_c2 = sem(name + "_c2")
            s_y = sem(name + "_y")
            s_x2 = sem(name + "_x2")
            with nc.Block() as block:
                @block.sync
                def _(sp):
                    with sp.Fori(0, BATCH) as b:
                        for u in range(2):
                            sp.wait_ge(s_T, 8 * b + BASE)
                            sp.dma_start(oT[:, u, :, :],
                                         o_d[bass.ds(b * NQ, NQ), :, u * CH:(u + 1) * CH]
                                         .rearrange("n p t -> p n t")).then_inc(s_ld[u], 16)
                            sp.wait_ge(s_x2, 2 * b + BASE)
                            sp.dma_start(xx[:, u, :, :],
                                         xx_d[bass.ds(b * T + u * CH, CH), :].rearrange("(t p) c -> p t c", p=P))\
                                .then_inc(s_xx[u], 16)

                @block.tensor
                def _(pe):
                    with pe.Fori(0, BATCH) as b:
                        for u in range(2):
                            pe.wait_ge(s_ld[u], 16 * (b + 1) + BASE)
                            for t in range(CT):
                                pe.wait_ge(s_on, 8 * b + 4 * u + t + 1 + BASE)
                                for q in range(NQ):
                                    i = nc.tensor.transpose(ps[:, t % 2, q * P:(q + 1) * P],
                                                            oT[:, u, q, t * P:(t + 1) * P], identity[:, :])
                                i.then_inc(s_T, 1)
                        for u in range(2):
                            pe.wait_ge(s_on, 8 * b + 4 * u + 4 + 2 + BASE)
                            pe.wait_ge(s_c2, 4 * b + BASE)
                            for half in range(2):
                                for t in range(CT):
                                    i = nc.tensor.transpose(ps[:, 2 + 2 * u + half, t * P:(t + 1) * P],
                                                            on[:, u, t, half * P:(half + 1) * P], identity[:, :])
                                i.then_inc(s_T2, 1)
                        for u in range(2):
                            pe.wait_ge(s_c2, 4 * b + 2 * u + 2 + BASE)
                            pe.wait_ge(s_x2, 2 * b + BASE)
                            for t in range(CT):
                                for half in range(2):
                                    i = nc.tensor.matmul(ps[:, 6 + u, t * P:(t + 1) * P],
                                                         onT[:, u, half, t * P:(t + 1) * P], wout_m[:, half, :],
                                                         start=(half == 0), stop=(half == 1))
                            i.then_inc(s_y, 1)

                @block.scalar
                def _(act):
                    with act.Fori(0, BATCH) as b:
                        for u in range(2):
                            for half in range(2):
                                act.wait_ge(s_T2, 4 * b + 2 * u + half + 1 + BASE)
                                act.wait_ge(s_y, 2 * b + BASE)
                                nc.scalar.activation(onT[:, u, half, :], ps[:, 2 + 2 * u + half, :], ACT.Copy)\
                                    .then_inc(s_c2, 1)

                @block.vector
                def _(dve):
                    dve.sem_inc(s_on, 2)
                    with dve.Fori(0, BATCH) as b:
                        for u in range(2):
                            dve.wait_ge(s_T2, 4 * b + BASE)
                            for t in range(CT):
                                dve.wait_ge(s_T, 8 * b + 4 * u + t + 1 + BASE)
                                o3 = ps[:, t % 2, :].rearrange("p (h w) -> p h w", w=VW)
                                nc.vector.reciprocal(rden[:, u, t, :], o3[:, :, LAT]).then_inc(s_rd, 1)
                                dve.wait_ge(s_rd, 8 * b + 4 * u + t + 1 + BASE)
                                nc.vector.tensor_tensor(
                                    on[:, u, t, :].rearrange("p (h d) -> p h d", d=LAT), o3[:, :, 0:LAT],
                                    rden[:, u, t, :].unsqueeze(2).to_broadcast([P, HEADS, LAT]), ALU.mult)\
                                    .then_inc(s_on, 1)
                        for u in range(2):
                            dve.wait_ge(s_y, 2 * b + u + 1 + BASE)
                            dve.wait_ge(s_xx[u], 16 * (b + 1) + BASE)
                            nc.vector.tensor_tensor(
                                tiles_of(x2_res, b, u), ps[:, 6 + u, :].rearrange("p (t c) -> p t c", c=C),
                                xx[:, u, :, :], ALU.add).then_inc(s_x2, 1)

        def experts():
            name = "me"
            area_at[0] = 0
            norm = Norm(name + "ln")
            rms = RootMean(name + "rm")
            GP = PAIRS + 1
            xr = work(2, CT, C)
            xrT = work(2, CH)
            prob = work(2, CT, EXPERTS)
            red = work(2, CT)
            cmp1 = work(2, CT, EXPERTS, EXPERTS)
            cmp2 = work(2, CT, EXPERTS, EXPERTS)
            rank = work(2, CT, EXPERTS)
            comb = work(2, CT, EXPERTS)
            combT = work(2, CH)
            silu = work(2, CH)
            hT = work(2, GP, CH)
            ffn = work(2, CT, C)
            s_T = sem(name + "_T")
            s_xT = sem(name + "_xT")
            s_lg = sem(name + "_lg")
            s_g = sem(name + "_g")
            s_gs = sem(name + "_gs")
            s_ex = sem(name + "_ex")
            s_cT = sem(name + "_cT")
            s_cc = sem(name + "_cc")
            s_gu = sem(name + "_gu")
            s_cb = sem(name + "_cb")
            s_si = sem(name + "_si")
            s_h = sem(name + "_h")
            s_hc = sem(name + "_hc")
            s_z = sem(name + "_z")
            s_ff = sem(name + "_ff")
            s_res = sem(name + "_res")
            GATE = 12
            with nc.Block() as block:
                @block.scalar
                def _(act):
                    with act.Fori(0, BATCH) as b:
                        for u in range(2):
                            rms.squares(act, b, u, tiles_of(x2_res, b, u))
                        for u in range(2):
                            rms.apply(act, b, u, tiles_of(x2_res, b, u), xr[:, u, :, :], (s_T, 2 * b))
                        for u in range(2):
                            act.wait_ge(s_T, 2 * b + u + 1 + BASE)
                            act.wait_ge(s_gu, 2 * GP * b + BASE)
                            nc.scalar.activation(xrT[:, u, :], ps[:, 0, :], ACT.Copy, scale=w_sb["ln2"][:, 0:1])\
                                .then_inc(s_xT, 1)
                        for u in range(2):
                            act.wait_ge(s_g, GATE * (2 * b + u) + 3 + BASE)
                            nc.scalar.activation(prob[:, u, :, :], prob[:, u, :, :], ACT.Exp).then_inc(s_ex, 1)
                        for u in range(2):
                            act.wait_ge(s_cT, 2 * b + u + 1 + BASE)
                            nc.scalar.activation(combT[0:EXPERTS, u, :], ps[0:EXPERTS, 1, :], ACT.Copy)\
                                .then_inc(s_cc, 1)
                        for u in range(2):
                            for j in range(GP):
                                n = 2 * GP * b + GP * u + j
                                rows = P if j < PAIRS else INNER
                                act.wait_ge(s_gu, n + 1 + BASE)
                                act.wait_ge(s_h, n + 1 + BASE)
                                nc.scalar.activation(silu[0:rows, (GP * u + j) % 2, :],
                                                     ps[0:rows, 2 + (GP * u + j) % 2, :], ACT.Silu).then_inc(s_si, 1)

                @block.gpsimd
                def _(pool):
                    pool.sem_inc(rms.s_go, 1)
                    with pool.Fori(0, BATCH) as b:
                        for u in range(2):
                            rms.inverse(pool, b, u)
                        for u in range(2):
                            norm.inverse(pool, b, u)

                @block.tensor
                def _(pe):
                    with pe.Fori(0, BATCH) as b:
                        for u in range(2):
                            pe.wait_ge(rms.s_out, 2 * b + u + 1 + BASE)
                            pe.wait_ge(s_xT, 2 * b + u + BASE)
                            transpose_chunk(0, xr[:, u, :, :]).then_inc(s_T, 1)
                        for u in range(2):
                            pe.wait_ge(s_xT, 2 * b + u + 1 + BASE)
                            pe.wait_ge(s_ff, 2 * b + BASE)
                            for t in range(CT):
                                i = nc.tensor.matmul(ps[:, 6 + u, t * EXPERTS:(t + 1) * EXPERTS],
                                                     xrT[:, u, t * P:(t + 1) * P], w_sb["wgate"][:, :],
                                                     start=True, stop=True)
                            i.then_inc(s_lg, 1)
                        for u in range(2):
                            pe.wait_ge(s_g, GATE * (2 * b + u + 1) + BASE)
                            pe.wait_ge(s_cc, 2 * b + u + BASE)
                            for t in range(CT):
                                i = nc.tensor.transpose(ps[0:EXPERTS, 1, t * P:(t + 1) * P], comb[:, u, t, :],
                                                        identity[:, :])
                            i.then_inc(s_cT, 1)
                        for u in range(2):
                            pe.wait_ge(s_cc, 2 * b + u + 1 + BASE)
                            for j in range(GP):
                                n = 2 * GP * b + GP * u + j
                                rows = P if j < PAIRS else INNER
                                r = (GP * u + j) % 2
                                pe.wait_ge(s_h, n + 1 + BASE)
                                nc.tensor.matmul(ps[0:rows, 2 + r, :], w_sb["wg"][:, j * P:j * P + rows],
                                                 xrT[:, u, :], start=True, stop=True)
                                nc.tensor.matmul(ps[0:rows, 4 + r, :], w_sb["wu"][:, j * P:j * P + rows],
                                                 xrT[:, u, :], start=True, stop=True).then_inc(s_gu, 1)
                                if j < PAIRS:
                                    pe.wait_ge(s_hc, PAIRS * (2 * b + u) + j + BASE)
                                    nc.tensor.matmul(ps[:, 0, :], w_sb["spread"][:, j * P:(j + 1) * P],
                                                     combT[0:EXPERTS, u, :], start=True, stop=True).then_inc(s_cb, 1)
                        for u in range(2):
                            pe.wait_ge(s_hc, PAIRS * (2 * b + u + 1) + BASE)
                            pe.wait_ge(s_h, GP * (2 * b + u + 1) + 2 + BASE)
                            for t in range(CT):
                                for j in range(GP):
                                    rows = P if j < PAIRS else INNER
                                    i = nc.tensor.matmul(ps[:, 6 + u, t * P:(t + 1) * P],
                                                         hT[0:rows, u, j, t * P:(t + 1) * P],
                                                         w_sb["wd"][0:rows, j, :], start=(j == 0), stop=(j == GP - 1))
                            i.then_inc(s_z, 1)

                @block.vector
                def _(dve):
                    dve.sem_inc(s_h, 2)

                    def gate(b, u):
                        c = [GATE * (2 * b + u)]

                        def step(i):
                            i.then_inc(s_g, 1)
                            c[0] = c[0] + 1
                            dve.wait_ge(s_g, c[0] + BASE)

                        pr = prob[:, u, :, :]
                        shape = [P, CT, EXPERTS]
                        big = [P, CT, EXPERTS, EXPERTS]
                        dve.wait_ge(s_lg, 2 * b + u + 1 + BASE)
                        step(nc.vector.tensor_tensor(
                            pr, ps[:, 6 + u, 0:CT * EXPERTS].rearrange("p (t e) -> p t e", t=CT),
                            w_sb["bias"][:, :].unsqueeze(1).to_broadcast(shape), ALU.add))
                        step(nc.vector.tensor_reduce(red[:, u, :], pr, AX_X, ALU.max))
                        nc.vector.tensor_tensor(pr, pr, red[:, u, :].unsqueeze(2).to_broadcast(shape), ALU.subtract)\
                            .then_inc(s_g, 1)
                        c[0] = c[0] + 1
                        dve.wait_ge(s_ex, 2 * b + u + 1 + BASE)
                        step(nc.vector.tensor_reduce(red[:, u, :], pr, AX_X, ALU.add))
                        step(nc.vector.reciprocal(red[:, u, :], red[:, u, :]))
                        step(nc.vector.tensor_tensor(pr, pr, red[:, u, :].unsqueeze(2).to_broadcast(shape), ALU.mult))
                        other = pr.unsqueeze(2).to_broadcast(big)
                        own = pr.unsqueeze(3).to_broadcast(big)
                        nc.vector.tensor_tensor(cmp1[:, u, :, :, :], other, own, ALU.is_gt)
                        step(nc.vector.tensor_tensor(cmp2[:, u, :, :, :], other, own, ALU.is_equal))
                        step(nc.vector.tensor_tensor(
                            cmp2[:, u, :, :, :], cmp2[:, u, :, :, :],
                            w_sb["earlier"][:, :].rearrange("p (a b) -> p a b", a=EXPERTS)
                            .unsqueeze(1).to_broadcast(big), ALU.mult))
                        step(nc.vector.tensor_tensor(cmp1[:, u, :, :, :], cmp1[:, u, :, :, :], cmp2[:, u, :, :, :],
                                                     ALU.add))
                        step(nc.vector.tensor_reduce(rank[:, u, :, :], cmp1[:, u, :, :, :], AX_X, ALU.add))
                        step(nc.vector.scalar_tensor_tensor(out=comb[:, u, :, :], in0=rank[:, u, :, :],
                                                            scalar=TOPK - 0.5, in1=pr, op0=ALU.is_lt, op1=ALU.mult))
                        nc.vector.tensor_reduce(red[:, u, :], comb[:, u, :, :], AX_X, ALU.add).then_inc(s_gs, 1)
                        dve.wait_ge(s_gs, 2 * (2 * b + u) + 1 + BASE)
                        nc.vector.reciprocal(red[:, u, :], red[:, u, :]).then_inc(s_gs, 1)
                        dve.wait_ge(s_gs, 2 * (2 * b + u) + 2 + BASE)
                        nc.vector.tensor_tensor(comb[:, u, :, :], comb[:, u, :, :],
                                                red[:, u, :].unsqueeze(2).to_broadcast(shape), ALU.mult)\
                            .then_inc(s_g, 1)

                    with dve.Fori(0, BATCH) as b:
                        for u in range(2):
                            dve.wait_ge(s_cT, 2 * b + BASE)
                            gate(b, u)
                        for u in range(2):
                            dve.wait_ge(s_z, 2 * b + BASE)
                            for j in range(GP):
                                n = 2 * GP * b + GP * u + j
                                rows = P if j < PAIRS else INNER
                                r = (GP * u + j) % 2
                                dve.wait_ge(s_si, n + 1 + BASE)
                                nc.vector.tensor_tensor(hT[0:rows, u, j, :], ps[0:rows, 4 + r, :],
                                                        silu[0:rows, r, :], ALU.mult).then_inc(s_h, 1)
                                if j < PAIRS:
                                    dve.wait_ge(s_h, n + 1 + 2 + BASE)
                                    dve.wait_ge(s_cb, PAIRS * (2 * b + u) + j + 1 + BASE)
                                    nc.vector.tensor_tensor(hT[:, u, j, :], ps[:, 0, :], hT[:, u, j, :], ALU.mult)\
                                        .then_inc(s_hc, 1)
                        for u in range(2):
                            dve.wait_ge(s_z, 2 * b + u + 1 + BASE)
                            dve.wait_ge(s_res, 2 * b + BASE)
                            nc.vector.tensor_tensor(ffn[:, u, :, :],
                                                    ps[:, 6 + u, :].rearrange("p (t c) -> p t c", c=C),
                                                    tiles_of(x2_res, b, u), ALU.add).then_inc(s_ff, 1)
                            dve.wait_ge(s_ff, 2 * b + u + 1 + BASE)
                            norm.stats(dve, b, u, ffn[:, u, :, :])
                        for u in range(2):
                            norm.apply(dve, b, u, ffn[:, u, :, :], ffn[:, u, :, :])
                            dve.wait_ge(norm.s_out, 2 * b + u + 1 + BASE)
                            nc.vector.tensor_tensor(tiles_of(x_res, b, u), tiles_of(x_res, b, u), ffn[:, u, :, :],
                                                    ALU.add).then_inc(s_res, 1)

        def low_rank_ffn():
            name = "lf"
            area_at[0] = 0
            norm = Norm(name + "a")
            norm2 = Norm(name + "b")
            FB = DFF // P
            xn = work(2, CT, C)
            xnT = work(2, CH)
            pT = work(2, CH)
            hT = work(2, FB, CH)
            qT = work(2, CH)
            y = work(2, CT, C)
            s_T = sem(name + "_T")
            s_xT = sem(name + "_xT")
            s_p = sem(name + "_p")
            s_pc = sem(name + "_pc")
            s_h = sem(name + "_h")
            s_gl = sem(name + "_gl")
            s_q = sem(name + "_q")
            s_qc = sem(name + "_qc")
            s_y = sem(name + "_y")
            s_yb = sem(name + "_yb")
            s_res = sem(name + "_res")
            s_st = [sem(f"{name}_st{u}") for u in range(2)]
            with nc.Block() as block:
                @block.vector
                def _(dve):
                    with dve.Fori(0, BATCH) as b:
                        for u in range(2):
                            norm.stats(dve, b, u, tiles_of(x_res, b, u))
                        for u in range(2):
                            dve.wait_ge(s_T, 2 * b + BASE)
                            norm.apply(dve, b, u, tiles_of(x_res, b, u), xn[:, u, :, :])
                        for u in range(2):
                            dve.wait_ge(s_p, 2 * b + u + 1 + BASE)
                            dve.wait_ge(s_h, 2 * FB * b + BASE)
                            nc.vector.tensor_copy(pT[0:RANK, u, :], ps[0:RANK, 2, :]).then_inc(s_pc, 1)
                        for u in range(2):
                            dve.wait_ge(s_q, 2 * b + u + 1 + BASE)
                            dve.wait_ge(s_y, 2 * b + BASE)
                            nc.vector.tensor_copy(qT[0:RANK, u, :], ps[0:RANK, 5, :]).then_inc(s_qc, 1)
                        for u in range(2):
                            dve.wait_ge(s_y, 2 * b + u + 1 + BASE)
                            dve.wait_ge(s_res, 2 * b + BASE)
                            nc.vector.tensor_tensor(y[:, u, :, :],
                                                    ps[:, 6 + u, :].rearrange("p (t c) -> p t c", c=C),
                                                    w_sb["b2"][:, :].unsqueeze(1).to_broadcast([P, CT, C]), ALU.add)\
                                .then_inc(s_yb, 1)
                            dve.wait_ge(s_yb, 2 * b + u + 1 + BASE)
                            norm2.stats(dve, b, u, y[:, u, :, :])
                        for u in range(2):
                            norm2.apply(dve, b, u, y[:, u, :, :], y[:, u, :, :])
                            dve.wait_ge(norm2.s_out, 2 * b + u + 1 + BASE)
                            nc.vector.tensor_tensor(tiles_of(x_res, b, u), tiles_of(x_res, b, u), y[:, u, :, :],
                                                    ALU.add).then_inc(s_res, 1)

                @block.gpsimd
                def _(pool):
                    with pool.Fori(0, BATCH) as b:
                        for u in range(2):
                            norm.inverse(pool, b, u)
                        for u in range(2):
                            norm2.inverse(pool, b, u)

                @block.tensor
                def _(pe):
                    with pe.Fori(0, BATCH) as b:
                        for u in range(2):
                            pe.wait_ge(norm.s_out, 2 * b + u + 1 + BASE)
                            pe.wait_ge(s_xT, 2 * b + BASE)
                            transpose_chunk(u, xn[:, u, :, :]).then_inc(s_T, 1)
                        for u in range(2):
                            pe.wait_ge(s_xT, 2 * b + u + 1 + BASE)
                            pe.wait_ge(s_pc, 2 * b + u + BASE)
                            nc.tensor.matmul(ps[0:RANK, 2, :], w_sb["u1"][:, :], xnT[:, u, :], start=True, stop=True)\
                                .then_inc(s_p, 1)
                        for u in range(2):
                            pe.wait_ge(s_pc, 2 * b + u + 1 + BASE)
                            for f in range(FB):
                                n = 2 * FB * b + FB * u + f
                                pe.wait_ge(s_gl, n + 1 + BASE)
                                nc.tensor.matmul(ps[:, 3 + f % 2, :], w_sb["v1"][:, f * P:(f + 1) * P],
                                                 pT[0:RANK, u, :], start=True, stop=True).then_inc(s_h, 1)
                        for u in range(2):
                            pe.wait_ge(s_qc, 2 * b + u + BASE)
                            pe.wait_ge(s_gl, FB * (2 * b + u + 1) + 2 + BASE)
                            for f in range(FB):
                                i = nc.tensor.matmul(ps[0:RANK, 5, :], w_sb["u2"][:, f, :], hT[:, u, f, :],
                                                     start=(f == 0), stop=(f == FB - 1))
                            i.then_inc(s_q, 1)
                        for u in range(2):
                            pe.wait_ge(s_qc, 2 * b + u + 1 + BASE)
                            pe.wait_ge(s_yb, 2 * b + BASE)
                            for t in range(CT):
                                i = nc.tensor.matmul(ps[:, 6 + u, t * P:(t + 1) * P],
                                                     qT[0:RANK, u, t * P:(t + 1) * P], w_sb["v2"][:, :],
                                                     start=True, stop=True)
                            i.then_inc(s_y, 1)

                @block.scalar
                def _(act):
                    act.sem_inc(s_gl, 2)
                    with act.Fori(0, BATCH) as b:
                        for u in range(2):
                            act.wait_ge(s_T, 2 * b + u + 1 + BASE)
                            act.wait_ge(s_p, 2 * b + BASE)
                            nc.scalar.activation(xnT[:, u, :], ps[:, u, :], ACT.Copy).then_inc(s_xT, 1)
                        for u in range(2):
                            act.wait_ge(s_q, 2 * b + BASE)
                            for f in range(FB):
                                n = 2 * FB * b + FB * u + f
                                act.wait_ge(s_h, n + 1 + BASE)
                                nc.scalar.activation(hT[:, u, f, :], ps[:, 3 + f % 2, :], ACT.Gelu_apprx_tanh,
                                                     bias=w_sb["b1"][:, f:f + 1]).then_inc(s_gl, 1)

                @block.sync
                def _(sp):
                    with sp.Fori(0, BATCH) as b:
                        for u in range(2):
                            sp.wait_ge(s_res, 2 * b + u + 1 + BASE)
                            sp.dma_start(out.rearrange("b (t p) c -> p (b t) c", p=P)
                                         [:, bass.ds((b * HALVES + u) * CT, CT), :],
                                         tiles_of(x_res, b, u)).then_inc(s_st[u], 16)
                    for u in range(2):
                        sp.wait_ge(s_st[u], 16 * BATCH + BASE)

        end_phase()
        project_heads8("p0", w_sb["wq0"][:, :], w_sb["wk0"][:, :], w_sb["wv0"][:, :])
        end_phase()
        attention("a0", 8.0 ** -0.5, latent=False, has_max=False, clip=True)
        end_phase()
        finish_heads8("f0", w_sb["wout0"][:, :])
        end_phase()
        project_latent()
        end_phase()
        attention("am", 0.125, latent=True, has_max=True, clip=False)
        end_phase()
        finish_latent()
        end_phase()
        experts()
        end_phase()
        project_heads8("p1", w_sb["wq1"][:, :], w_sb["wk1"][:, :], w_sb["wv1"][:, :])
        end_phase()
        attention("a1", 8.0 ** -0.5, latent=False, has_max=True, clip=False)
        end_phase()
        finish_heads8("f1", None)
        end_phase()
        low_rank_ffn()
        end_phase()


def lay_out(inputs):
    a = {k: np.asarray(v) for k, v in inputs.items()}
    f = np.float32
    order = np.arange(C).reshape(NQ, 2, 2, 8).transpose(0, 2, 3, 1).reshape(-1)
    w0, w1 = a["L0_attn_Wqkv"].T, a["L1_attn_w_qkv"]
    c = {
        "wq0": w0[:, 0:C][:, order], "wk0": w0[:, C:2 * C][:, order], "wv0": w0[:, 2 * C:],
        "wq1": w1[:, 0:C][:, order], "wk1": w1[:, C:2 * C][:, order], "wv1": w1[:, 2 * C:],
        "wout0": a["L0_attn_Wout"].T,
    }
    wq = a["L0_ffn_Wq"].reshape(C, HEADS, 64)
    c["wq_nope"] = wq[:, :, 0:32].transpose(2, 1, 0)
    rope = wq[:, :, 32:].reshape(C, NQ, QUAD, 32).transpose(0, 1, 3, 2)
    swap = np.arange(32).reshape(16, 2)[:, ::-1].reshape(-1)
    c["wq_rope"] = rope.reshape(C, NQ, P)
    c["wq_rope_sw"] = rope[:, :, swap].reshape(C, NQ, P)
    c["wkva"] = a["L0_ffn_Wkva"]
    c["wkva_sw"] = np.concatenate([a["L0_ffn_Wkva"][:, 0:LAT], a["L0_ffn_Wkva"][:, LAT + swap]], axis=1)
    wkvb = a["L0_ffn_Wkvb"].reshape(LAT, HEADS, 32)
    z = np.zeros((32, HEADS, P), f)
    for h in range(HEADS):
        z[:, h, (h % 8) * LAT:(h % 8 + 1) * LAT] = wkvb[:, h].T
    c["wkvb_z"] = z
    c["wo_nope"] = a["L0_ffn_Wo"].reshape(HEADS, 64, C)[:, 0:32].transpose(1, 0, 2)
    c["ln1"] = a["L0_ffn_w_ln1"].reshape(C, 1)
    c["ln2"] = a["L0_ffn_w_ln2"].reshape(C, 1)
    c["wgate"] = a["L0_ffn_Wgate"]
    c["bias"] = np.broadcast_to(a["L0_ffn_expert_bias"], (P, EXPERTS))
    c["wg"] = np.concatenate([a["L0_ffn_Wg"], a["L0_ffn_sWg"]]).transpose(1, 0, 2).reshape(C, -1)
    c["wu"] = np.concatenate([a["L0_ffn_Wu"], a["L0_ffn_sWu"]]).transpose(1, 0, 2).reshape(C, -1)
    wd = np.concatenate([a["L0_ffn_Wd"], a["L0_ffn_sWd"]]).reshape(-1, C)
    wd = np.concatenate([wd, np.zeros((INNER, C), f)])
    c["wd"] = wd.reshape(PAIRS + 1, P, C).transpose(1, 0, 2)
    c["u1"], c["v1"], c["v2"] = a["L1_ffn_U1"], a["L1_ffn_V1"], a["L1_ffn_V2"]
    c["u2"] = a["L1_ffn_U2"].reshape(DFF // P, P, RANK).transpose(1, 0, 2)
    c["b1"] = a["L1_ffn_b1"].reshape(DFF // P, P).T
    c["b2"] = np.broadcast_to(a["L1_ffn_b2"], (P, C))
    ang = np.outer(np.arange(T, dtype=f), f(1.0) / f(100000.0) ** (np.arange(0, 32, 2, dtype=f) / f(32))).T
    cos, sin = np.repeat(np.cos(ang), 2, 0), np.repeat(np.sin(ang), 2, 0)
    sin[0::2] = -sin[0::2]
    c["cos_q"], c["sin_q"] = np.repeat(cos, QUAD, 0), np.repeat(sin, QUAD, 0)
    c["cos_k"] = np.concatenate([np.ones((LAT, T), f), cos])
    c["sin_k"] = np.concatenate([np.zeros((LAT, T), f), sin])
    e = np.arange(EXPERTS)
    c["earlier"] = np.broadcast_to((e[None, :] < e[:, None]).astype(f).reshape(-1), (P, EXPERTS * EXPERTS))
    c["spread"] = np.repeat(np.eye(EXPERTS, dtype=f), INNER, axis=1)
    return {k: np.ascontiguousarray(v) for k, v in c.items()}


def kernel(**inputs):
    import concourse.bacc as bacc
    from concourse.bass_utils import run_bass_kernel_spmd as run

    nc = bacc.Bacc("TRN2", target_bir_lowering=False, num_devices=1)
    arrays = {"in_x": np.ascontiguousarray(inputs["L0_attn_x"])}
    x = nc.dram_tensor("in_x", arrays["in_x"].shape, F32, kind="ExternalInput").ap()
    consts = {}
    for n, v in lay_out(inputs).items():
        arrays["in_" + n] = v
        consts[n] = nc.dram_tensor("in_" + n, v.shape, F32, kind="ExternalInput").ap()
    out = nc.dram_tensor("out", (BATCH, T, C), F32, kind="ExternalOutput").ap()
    build(nc, {"x": x}, consts, out)
    return run(nc, [arrays], core_ids=[0]).results[0]["out"]
```

```python
from contextlib import ExitStack

import concourse.bass as bass
from concourse import mybir
import numpy as np

P = 128
F32 = mybir.dt.float32
BF16 = mybir.dt.bfloat16
ALU = mybir.AluOpType
ACT = mybir.ActivationFunctionType
AX_X = mybir.AxisListType.X

BATCH, T, C = 4, 1024, 128
TOK = BATCH * T
TILES = TOK // P
CH = 512
CT = CH // P
HALVES = T // CH
KB = T // P
HEADS, QUAD = 16, 4
NQ = HEADS // QUAD
ITEMS = BATCH * NQ
UNIT = CH
ROWS_P = (KB * (KB + 1) // 2) * P // UNIT
UNITS = ROWS_P * QUAD
VW = 32
EPS = 1e-5
BASE = 1
NEG = -1e30
QTERM = (0, 0, 0, 1, 1, 2)
KTERM = (0, 1, 2, 0, 1, 0)
LAT, ROPE, MD = 16, 32, 48
EXPERTS, TOPK, INNER = 8, 2, 64
PAIRS = EXPERTS // 2
RANK, DFF = 32, 512


def key_major_units():
    blocks = [(k, q) for k in range(KB) for q in range(k, KB)]
    units = []
    for g in range(ROWS_P):
        segs = []
        for off, (k, q) in enumerate(blocks[4 * g:4 * g + 4]):
            if segs and segs[-1][0] == k:
                segs[-1][2] += 1
            else:
                segs.append([k, q, 1, off])
        units.append([tuple(s) for s in segs])
    return units


M_ORDER = (7, 3, 6, 0, 5, 1, 4, 2)


def query_major_units():
    blocks = [(q, k) for q in M_ORDER for k in range(q + 1)]
    units = []
    for g in range(ROWS_P):
        segs = []
        for off, (q, k) in enumerate(blocks[4 * g:4 * g + 4]):
            if segs and segs[-1][0] == q:
                segs[-1][2] += 1
            else:
                segs.append([q, k, 1, off, 1 if k >= 4 else 0])
        units.append([tuple(s) for s in segs])
    return units


S_UNITS = key_major_units()
M_UNITS = query_major_units()


def build(nc, ins, consts, out):
    stack = ExitStack()
    with stack:
        def sb(name, shape, dt=F32):
            return stack.enter_context(nc.sbuf_tensor(name, shape, dt))

        phase_sems = []

        def sem(name):
            phase_sems.append(nc.alloc_semaphore(name=name))
            nc.sync.sem_inc(phase_sems[-1], BASE)
            return phase_sems[-1]

        def end_phase():
            nc.clear_and_free_semaphores(phase_sems)
            phase_sems.clear()
            nc.all_engine_barrier()

        def scratch(name, shape, dt=F32):
            return nc.dram_tensor(name, shape, dt, kind="Internal").ap()

        def wait_alone(eng, semaphore, value, *others):
            pairs = [(x, v + BASE if isinstance(v, int) else eng.to_reg(v + BASE))
                     for x, v in ((semaphore, value), *others)]
            eng.wait_ge(semaphore, BASE + 1)
            for x, v in pairs:
                eng.wait_ge(x, v)

        q8_d = scratch("q8_d", [ITEMS, 2, 3, 8, 2, T], BF16)
        k8_d = scratch("k8_d", [ITEMS, 2, 3, 8, 2, T], BF16)
        v8_d = scratch("v8_d", [TOK, HEADS * VW])
        qm_d = scratch("qm_d", [ITEMS, 3, MD, QUAD, T], BF16)
        vm_d = scratch("vm_d", [TOK, VW])
        mx_d = scratch("mx_d", [ITEMS, 3, QUAD, T], BF16)
        o_d = scratch("o_d", [ITEMS, P, T])
        xx_d = scratch("xx_d", [TOK, C])

        x_res = sb("x_res", [P, TILES, C])
        identity = sb("identity", [P, P])
        ident_bf = sb("ident_bf", [P, P], BF16)
        causal_bf = sb("causal_bf", [P, P], BF16)
        zero_f = sb("zero_f", [P, P])
        minus_half = sb("minus_half", [P, CT])

        FOLDED = ("wq_nope", "wkvb_z", "wo_nope")
        TABLES = ("cos_q", "sin_q", "cos_k", "sin_k")
        w_sb = {n: sb("w_" + n, list(a.shape)) for n, a in consts.items() if n not in FOLDED + TABLES}
        wabs = sb("wabs", [C, NQ // 2, 2, LAT, QUAD])
        wout_m = sb("wout_m", [P, 2, C])
        ps = stack.enter_context(nc.psum_tensor("ps", [P, 8, UNIT], F32))

        pmax = sb("pmax", [P, QUAD, KB, 2])
        mx_sb = sb("mx_sb", [P, 2, QUAD * KB])
        MR = QUAD * KB
        mx_turned = sb("mx_turned", [P, MR])
        m_parts = sb("m_parts", [P, 2, 3, MR], BF16)
        m_rest = sb("m_rest", [P, MR])
        o_sb = sb("o_sb", [P, 1, T])
        kterm_d = [scratch(f"kterm{c}_d", [BATCH, 2 * MD, T], BF16) for c in range(3)]

        NB = 4
        q_buf = sb("q_buf", [P, NB, 3 * QUAD * T], BF16)
        k_buf = sb("k_buf", [P, NB, 3 * T], BF16)
        v_buf = sb("v_buf", [P, NB, KB * QUAD * VW])
        pr_buf = sb("pr_buf", [P, 12, UNIT])
        area = q_buf[:, :, :].rearrange("p a b -> p (a b)").bitcast(F32)
        area_at = [0]

        def work(*shape, dt=F32, parts=P):
            n = int(np.prod(shape))
            words = n if dt == F32 else (n + 1) // 2
            a = area[0:parts, area_at[0]:area_at[0] + words]
            area_at[0] += words
            assert area_at[0] <= 24576
            if dt != F32:
                a = a.bitcast(dt)
            names = "abcde"[:len(shape)]
            if len(shape) > 1:
                a = a.rearrange("p (" + " ".join(names) + ") -> p " + " ".join(names),
                                **{k: v for k, v in zip(names[1:], shape[1:])})
            return a

        for n in FOLDED:
            w_sb[n] = work(HEADS, P, parts=32)
        ld_w = sem("ld_w")
        c_zero = sem("c_zero")
        c_const = sem("c_const")
        c_bf = sem("c_bf")
        fold_mm = sem("fold_mm")
        with nc.Block() as block:
            @block.sync
            def _(sp):
                sp.dma_start(x_res[:, :, :], ins["x"].rearrange("b (t p) c -> p (b t) c", p=P)).then_inc(ld_w, 16)
                for n, w in w_sb.items():
                    sp.dma_start(w[tuple(slice(None) for _ in w.shape)], consts[n]).then_inc(ld_w, 16)
                sp.wait_ge(ld_w, 16 * (1 + len(w_sb)) + BASE)

            @block.gpsimd
            def _(pool):
                nc.gpsimd.memset(zero_f[:, :], 0.0).then_inc(c_zero, 1)
                nc.gpsimd.memset(minus_half[:, :], -0.5).then_inc(c_const, 1)
                pool.wait_ge(c_zero, 1 + BASE)
                nc.gpsimd.affine_select(out=identity[:, :], in_=zero_f[:, :], compare_op=ALU.not_equal, fill=1.0,
                                        base=0, pattern=[[-1, P]], channel_multiplier=1).then_inc(c_const, 1)
                pool.wait_ge(c_const, 2 + BASE)
                nc.gpsimd.tensor_copy(ident_bf[:, :], identity[:, :]).then_inc(c_const, 1)
                nc.gpsimd.affine_select(out=zero_f[:, :], in_=zero_f[:, :], compare_op=ALU.is_ge, fill=NEG,
                                        base=0, pattern=[[-1, P]], channel_multiplier=1).then_inc(c_const, 1)
                pool.wait_ge(c_const, 4 + BASE)
                nc.gpsimd.tensor_copy(causal_bf[:, :], zero_f[:, :]).then_inc(c_bf, 1)

            @block.tensor
            def _(pe):
                pe.wait_ge(ld_w, 16 * (1 + len(w_sb)) + BASE)
                for h in range(HEADS):
                    mm = nc.tensor.matmul(ps[:, 0, h * LAT:(h + 1) * LAT], w_sb["wq_nope"][:, h, :],
                                          w_sb["wkvb_z"][:, h, (h % 8) * LAT:(h % 8 + 1) * LAT],
                                          start=True, stop=True)
                mm.then_inc(fold_mm, 1)
                for half in range(2):
                    for h in range(8):
                        hh = 8 * half + h
                        mm = nc.tensor.matmul(ps[:, 1 + half, 0:C], w_sb["wkvb_z"][:, hh, :],
                                              w_sb["wo_nope"][:, hh, :], start=(h == 0), stop=(h == 7))
                mm.then_inc(fold_mm, 1)

            @block.vector
            def _(dve):
                dve.wait_ge(fold_mm, 1 + BASE)
                for half in range(2):
                    for qd in range(2):
                        nc.vector.tensor_copy(
                            wabs[:, half, qd, :, :],
                            ps[:, 0, (half * 8 + qd * 4) * LAT:(half * 8 + qd * 4 + 4) * LAT]
                            .rearrange("p (h r) -> p r h", h=QUAD))
                dve.wait_ge(fold_mm, 2 + BASE)
                nc.vector.tensor_copy(wout_m[:, 0, :], ps[:, 1, 0:C])
                nc.vector.tensor_copy(wout_m[:, 1, :], ps[:, 2, 0:C])

        def tiles_of(res, b, u):
            return res[:, bass.ds((b * HALVES + u) * CT, CT), :]

        class Norm:

            def __init__(self, name):
                self.bn = work(2, CT, 6)
                self.mv = work(2, CT, 2)
                self.ve = work(2, CT)
                self.rstd = work(2, CT)
                self.s_bn = sem(name + "_bn")
                self.s_mv = sem(name + "_mv")
                self.s_ve = sem(name + "_ve")
                self.s_rstd = sem(name + "_rstd")
                self.s_out = sem(name + "_out")

            def stats(self, dve, b, u, src):
                dve.wait_ge(self.s_ve, 2 * b + BASE)
                for t in range(CT):
                    i = nc.vector.bn_stats(self.bn[:, u, t, :], src[:, t, :])
                i.then_inc(self.s_bn, 1)
                wait_alone(dve, self.s_bn, 2 * b + u + 1)
                for t in range(CT):
                    i = nc.vector.bn_aggr(self.mv[:, u, t, :], self.bn[:, u, t, :])
                i.then_inc(self.s_mv, 1)

            def inverse(self, pool, b, u):
                wait_alone(pool, self.s_mv, 2 * b + u + 1, (self.s_out, 2 * b))
                nc.gpsimd.tensor_scalar(self.ve[:, u, :], self.mv[:, u, :, 1], EPS, None, ALU.add).then_inc(self.s_ve, 1)
                pool.wait_ge(self.s_ve, 2 * b + u + 1 + BASE)
                nc.gpsimd.tensor_tensor(self.rstd[:, u, :], self.ve[:, u, :], minus_half[:, :], ALU.pow)\
                    .then_inc(self.s_rstd, 1)

            def apply(self, dve, b, u, src, dst):
                dve.wait_ge(self.s_rstd, 2 * b + u + 1 + BASE)
                for t in range(CT):
                    i = nc.vector.tensor_scalar(dst[:, t, :], src[:, t, :], self.mv[:, u, t, 0:1],
                                                self.rstd[:, u, t:t + 1], ALU.subtract, ALU.mult)
                i.then_inc(self.s_out, 1)

        class RootMean:

            def __init__(self, name):
                self.junk = work(2, CT, C)
                self.ms = work(2, CT)
                self.ve = work(2, CT)
                self.rinv = work(2, CT)
                self.s_go = sem(name + "_go")
                self.s_ms = sem(name + "_ms")
                self.s_ve = sem(name + "_ve")
                self.s_rinv = sem(name + "_rinv")
                self.s_out = sem(name + "_out")

            def squares(self, act, b, u, src):
                used = act.to_reg(2 * b + BASE)
                act.wait_ge(self.s_go, 1 + BASE)
                act.wait_ge(self.s_ve, used)
                for t in range(CT):
                    i = nc.scalar.activation(self.junk[:, u, t, :], src[:, t, :], ACT.Square, scale=float(C) ** -0.5,
                                             accum_out=self.ms[:, u, t:t + 1])
                i.then_inc(self.s_ms, 1)

            def inverse(self, pool, b, u):
                wait_alone(pool, self.s_ms, 2 * b + u + 1, (self.s_out, 2 * b))
                nc.gpsimd.tensor_scalar(self.ve[:, u, :], self.ms[:, u, :], EPS, None, ALU.add).then_inc(self.s_ve, 1)
                pool.wait_ge(self.s_ve, 2 * b + u + 1 + BASE)
                nc.gpsimd.tensor_tensor(self.rinv[:, u, :], self.ve[:, u, :], minus_half[:, :], ALU.pow)\
                    .then_inc(self.s_rinv, 1)

            def apply(self, act, b, u, src, dst, dst_free):
                wait_alone(act, self.s_rinv, 2 * b + u + 1, dst_free)
                for t in range(CT):
                    i = nc.scalar.activation(dst[:, t, :], src[:, t, :], ACT.Copy, scale=self.rinv[:, u, t:t + 1])
                i.then_inc(self.s_out, 1)

        def transpose_chunk(bank, src):
            for t in range(CT):
                i = nc.tensor.transpose(ps[:, bank, t * P:(t + 1) * P], src[:, t, :], identity[:, :])
            return i

        def run_chunks(eng, body, front=(), rest=None):
            for step in front:
                step(0, 0)
            with eng.Fori(0, BATCH - 1) as b:
                body(b, 0, (b, 1))
                body(b, 1, (b + 1, 0))
                if rest is not None:
                    rest(b)
            body(BATCH - 1, 0, (BATCH - 1, 1))
            body(BATCH - 1, 1, None)
            if rest is not None:
                rest(BATCH - 1)

        def project_heads8(name, wq, wk, wv):
            area_at[0] = 0
            norm = Norm(name + "ln")
            xn = work(2, CT, C)
            xnT = work(2, CH)
            rest = work(2, 2, CH)
            parts = work(2, 2, 3, CH, dt=BF16)
            v_pad = work(2, CT, HEADS, VW)
            s_pad = sem(name + "_pad")
            s_T = sem(name + "_T")
            s_xT = sem(name + "_xT")
            s_qk = sem(name + "_qk")
            s_v = sem(name + "_v")
            s_p1 = sem(name + "_p1")
            s_r1 = sem(name + "_r1")
            s_p2 = sem(name + "_p2")
            s_p3 = sem(name + "_p3")
            s_vp = sem(name + "_vp")
            s_st = [sem(name + f"_st{u}") for u in range(2)]
            with nc.Block() as block:
                @block.vector
                def _(dve):
                    nc.vector.memset(v_pad, 0.0).then_inc(s_pad, 1)
                    dve.wait_ge(s_pad, 1 + BASE)
                    nc.vector.memset(v_pad[:, :, :, :, 8:9], 1.0).then_inc(s_pad, 1)
                    with dve.Fori(0, BATCH) as b:
                        for u in range(2):
                            norm.stats(dve, b, u, tiles_of(x_res, b, u))
                        for u in range(2):
                            dve.wait_ge(s_T, 2 * b + BASE)
                            norm.apply(dve, b, u, tiles_of(x_res, b, u), xn[:, u, :, :])
                        for u in range(2):
                            dve.wait_ge(s_p3, 4 * b + BASE)
                            for s in range(2):
                                dve.wait_ge(s_p1, 4 * b + 2 * u + s + 1 + BASE)
                                nc.vector.tensor_tensor(rest[:, u, s, :], ps[:, 2 + 2 * s + u, :],
                                                        parts[:, u, s, 0, :], ALU.subtract).then_inc(s_r1, 1)
                            dve.wait_ge(s_v, 2 * b + u + 1 + BASE)
                            dve.wait_ge(s_st[u], 16 * 7 * b + BASE)
                            nc.vector.tensor_copy(v_pad[:, u, :, :, 0:8],
                                                  ps[:, 6 + u, :].rearrange("p (t h d) -> p t h d", t=CT, h=HEADS))\
                                .then_inc(s_vp, 1)

                @block.gpsimd
                def _(pool):
                    with pool.Fori(0, BATCH) as b:
                        for u in range(2):
                            norm.inverse(pool, b, u)
                        for u in range(2):
                            for s in range(2):
                                pool.wait_ge(s_p2, 4 * b + 2 * u + s + 1 + BASE)
                                nc.gpsimd.tensor_tensor(parts[:, u, s, 2, :], rest[:, u, s, :], parts[:, u, s, 1, :],
                                                        ALU.subtract).then_inc(s_p3, 1)

                @block.tensor
                def _(pe):
                    with pe.Fori(0, BATCH) as b:
                        for u in range(2):
                            pe.wait_ge(norm.s_out, 2 * b + u + 1 + BASE)
                            pe.wait_ge(s_xT, 2 * b + BASE)
                            transpose_chunk(u, xn[:, u, :, :]).then_inc(s_T, 1)
                        for u in range(2):
                            pe.wait_ge(s_xT, 2 * b + u + 1 + BASE)
                            pe.wait_ge(s_r1, 4 * b + BASE)
                            for s, w in enumerate((wq, wk)):
                                nc.tensor.matmul(ps[:, 2 + 2 * s + u, :], w, xnT[:, u, :], start=True, stop=True)\
                                    .then_inc(s_qk, 1)
                            pe.wait_ge(s_vp, 2 * b + BASE)
                            for t in range(CT):
                                mm = nc.tensor.matmul(ps[:, 6 + u, t * P:(t + 1) * P], xnT[:, u, t * P:(t + 1) * P],
                                                      wv, start=True, stop=True)
                            mm.then_inc(s_v, 1)

                @block.scalar
                def _(act):
                    with act.Fori(0, BATCH) as b:
                        for u in range(2):
                            act.wait_ge(s_T, 2 * b + u + 1 + BASE)
                            act.wait_ge(s_v, 2 * b + BASE)
                            nc.scalar.activation(xnT[:, u, :], ps[:, u, :], ACT.Copy).then_inc(s_xT, 1)
                        for u in range(2):
                            act.wait_ge(s_st[u], 16 * 7 * b + BASE)
                            for s in range(2):
                                act.wait_ge(s_qk, 4 * b + 2 * u + s + 1 + BASE)
                                nc.scalar.activation(parts[:, u, s, 0, :], ps[:, 2 + 2 * s + u, :], ACT.Copy)\
                                    .then_inc(s_p1, 1)
                            for s in range(2):
                                act.wait_ge(s_r1, 4 * b + 2 * u + s + 1 + BASE)
                                nc.scalar.activation(parts[:, u, s, 1, :], rest[:, u, s, :], ACT.Copy)\
                                    .then_inc(s_p2, 1)

                @block.sync
                def _(sp):
                    sp.wait_ge(s_pad, 2 + BASE)
                    with sp.Fori(0, BATCH) as b:
                        for u in range(2):
                            sp.wait_ge(s_vp, 2 * b + u + 1 + BASE)
                            sp.dma_start(
                                v8_d[bass.ds(b * T + u * CH, CH), :].rearrange("(t p) w -> p t w", p=P),
                                v_pad[:, u, :, :, :].rearrange("p t h w -> p t (h w)")).then_inc(s_st[u], 16)
                            sp.wait_ge(s_p3, 4 * b + 2 * u + 2 + BASE)
                            for s, d in enumerate((q8_d, k8_d)):
                                for part in range(3):
                                    sp.dma_start(
                                        d[bass.ds(b * NQ, NQ), :, part, :, :, u * CH:(u + 1) * CH]
                                        .rearrange("n a d h t -> n a (d h) t"),
                                        parts[:, u, s, part, :]).then_inc(s_st[u], 16)
                    for u in range(2):
                        sp.wait_ge(s_st[u], 16 * 7 * BATCH + BASE)

        def attention(name, scale, latent, has_max, clip):
            S_BANKS, M_BANKS = (4, 2) if has_max else (6, 0)
            LEAD = 12
            o_bank, s_bank0, m_bank0 = 0, 2, 6
            PRING = 3
            n_loads = (6 + 3 + 1) if latent else (2 * (6 + 3 + has_max) + 1)
            qs = q_buf[:, :, :].rearrange("p n (c h t) -> p n c h t", c=3, h=QUAD)
            ks = k_buf[:, :, :].rearrange("p n (c t) -> p n c t", c=3)
            if latent:
                vs = v_buf[:, :, 0:KB * VW].rearrange("p n (k w) -> p n k w", k=KB)
            else:
                vs = v_buf[:, :, :].rearrange("p n (k w) -> p n k w", k=KB)
            nm = name
            s_ld = [sem(f"{nm}_ld{s}") for s in range(NB)]
            s_mrow = [sem(f"{nm}_mrow{s}") for s in range(NB)]
            s_s = sem(nm + "_s")
            s_e = sem(nm + "_e")
            s_clip = sem(nm + "_clip")
            s_sel = sem(nm + "_sel")
            s_pv = sem(nm + "_pv")
            s_oc = sem(nm + "_oc")
            s_ost = sem(nm + "_ost")
            s_m = sem(nm + "_m")
            s_mr = sem(nm + "_mr")
            s_pm = sem(nm + "_pm")
            s_mT = sem(nm + "_mT")
            s_m1 = sem(nm + "_m1")
            s_m2 = sem(nm + "_m2")
            s_m3 = sem(nm + "_m3")
            s_m4 = sem(nm + "_m4")
            s_mst = sem(nm + "_mst")
            s_one = sem(nm + "_one")
            s_oneld = [sem(nm + f"_oneld{h}") for h in range(2)]
            s_pi = sem(nm + "_pi")
            s_clear = [sem(nm + f"_clear{e}") for e in range(2)]

            def clear(eng, slots, done):
                for s in slots:
                    eng.memset(q_buf[:, s, 0:6 * T].bitcast(F32), 0.0).then_inc(done, 1)
            minus_one = o_sb[0:3, 0, :].bitcast(BF16)

            diag = [[s for s in unit if s[0] == s[1]] for unit in S_UNITS]
            diags_before = [sum(QUAD * len(d) for d in diag[:g]) for g in range(ROWS_P + 1)]
            DIAGS = diags_before[-1]

            def m_events(t, last):
                k = t + LEAD
                off, k = 1 + k // UNITS, k % UNITS
                if last is not None and last + off >= ITEMS:
                    return []
                return [(off, k)]

            def slot(i, off=0):
                return (i + off) % NB

            def uses(b, i, off=0):
                return b + (i + off) // NB + 1

            def run_items(eng, item, first=None, rest=None):
                if first is not None:
                    first()
                item(0, 0, 0)
                with eng.Fori(0, BATCH - 1) as b:
                    for i in range(1, NQ + 1):
                        item(b, i, None)
                for i in range(1, NQ):
                    item(BATCH - 1, i, (BATCH - 1) * NQ + i)
                if rest is not None:
                    rest()

            def count_of(eng, b, i):
                if isinstance(b, int):
                    return b * NQ + i
                count = eng.alloc_register()
                eng.reg_mov(count, b * NQ + i)
                return eng.snap(count, donate=True, min_val=i, max_val=(BATCH - 2) * NQ + i)

            with nc.Block() as block:
                @block.sync
                def _(sp):
                    def load(b, i, off):
                        s = slot(i, off)
                        n = b * NQ + i + off
                        if latent:
                            for c in range(3):
                                for hf in range(2):
                                    t = 2 * c + hf
                                    sp.dma_start(qs[48 * hf:48 * hf + MD, s, c, :, :],
                                                 qm_d[bass.ds(n, 1), QTERM[t], :, :, :]
                                                 .rearrange("n r h t -> (n r) h t")).then_inc(s_ld[s], 16)
                            seq = b + (i + off) // NQ
                            for c in range(3):
                                sp.dma_start(ks[0:2 * MD, s, c, :],
                                             kterm_d[c][bass.ds(seq, 1), :, :]
                                             .rearrange("n r t -> (n r) t")).then_inc(s_ld[s], 16)
                            sp.dma_start(vs[:, s, :, :],
                                         vm_d[bass.ds(seq * T, T), :].rearrange("(k p) w -> p k w", p=P))\
                                .then_inc(s_ld[s], 16)
                        else:
                            seq = b + (i + off) // NQ
                            quad = (i + off) % NQ
                            for pr in range(2):
                                for t in range(6):
                                    sp.dma_start(qs[64 * pr + 8 * t:64 * pr + 8 * t + 8, s, 0, pr:QUAD:2, :],
                                                 q8_d[bass.ds(n, 1), pr, QTERM[t], :, :, :]
                                                 .rearrange("n d h t -> (n d) h t")).then_inc(s_ld[s], 16)
                                for t0, cnt in ((0, 3), (3, 2), (5, 1)):
                                    sp.dma_start(
                                        qs[64 * pr + 8 * t0:64 * pr + 8 * (t0 + cnt), s, 1, 0:2, :],
                                        k8_d[bass.ds(n, 1), pr, 0:cnt, :, :, :]
                                        .rearrange("n c d h t -> (n c d) h t")).then_inc(s_ld[s], 16)
                            if has_max:
                                for pr in range(2):
                                    sp.dma_start(qs[64 * pr + 48:64 * pr + 51, s, 0, pr:QUAD:2, :],
                                                 qs[51:54, s, 0, pr:QUAD:2, :])\
                                        .then_inc(s_ld[s], 16)
                            sp.dma_start(vs[:, s, :, :],
                                         v8_d[bass.ds(seq * T, T), quad * QUAD * VW:(quad + 1) * QUAD * VW]
                                         .rearrange("(k p) w -> p k w", p=P)).then_inc(s_ld[s], 16)

                    def maxima(b, i, off):
                        n = b * NQ + i + off
                        s = slot(i, off)
                        sp.wait_ge(s_m4, n + 1 + BASE)
                        for a in range(P // MR):
                            sp.dma_start(mx_d[bass.ds(n, 1), :, :, :]
                                         .rearrange("n c h (k a q) -> a (n h k) c q", a=P // MR, q=MR)[a],
                                         m_parts[MR * a:MR * (a + 1), (i + off) % 2, :, :]).then_inc(s_mst, 16)
                        sp.wait_ge(s_mst, 16 * (P // MR) * (n + 1) + BASE)
                        if latent:
                            for c in range(3):
                                sp.dma_start(qs[96:97, s, c, :, :], mx_d[bass.ds(n, 1), c, :, :])\
                                    .then_inc(s_mrow[s], 16)
                        else:
                            for pr in range(2):
                                sp.dma_start(qs[64 * pr + 48:64 * pr + 51, s, 0, pr:QUAD:2, :],
                                             mx_d[bass.ds(n, 1), :, :, :]
                                             .rearrange("n c (a r) t -> (n c) a r t", r=2)[:, :, pr, :])\
                                    .then_inc(s_mrow[s], 16)

                    def take_off_rows(half):
                        for s in (2 * half, 2 * half + 1):
                            for pr in range(2):
                                sp.dma_start(qs[64 * pr + 48:64 * pr + 51, s, 1, 0:2, :],
                                             minus_one.rearrange("p (a t) -> p a t", a=2))\
                                    .then_inc(s_oneld[half], 16)

                    def first():
                        if not latent:
                            sp.wait_ge(s_clear[0], 2 + BASE)
                        load(0, 0, 0)
                        load(0, 0, 1)
                        if has_max and not latent:
                            sp.wait_ge(s_one, 1 + BASE)
                            take_off_rows(0)
                        if not latent:
                            sp.wait_ge(s_clear[1], 2 + BASE)
                        if has_max and not latent:
                            take_off_rows(1)
                        if has_max:
                            maxima(0, 0, 0)

                    def item(b, i, last):
                        n = b * NQ + i
                        if last is None or last + 2 < ITEMS:
                            sp.wait_ge(s_s, UNITS * n + BASE)
                            load(b, i, 2)
                        if last != 0:
                            store(n - 1)
                        if has_max and (last is None or last + 1 < ITEMS):
                            maxima(b, i, 1)

                    def store(n):
                        sp.wait_ge(s_oc, n + 1 + BASE)
                        sp.dma_start(o_d[bass.ds(n, 1), :, :].rearrange("n p t -> (n p) t"), o_sb[:, 0, :])\
                            .then_inc(s_ost, 16)

                    run_items(sp, item, first, lambda: store(ITEMS - 1))
                    sp.wait_ge(s_ost, 16 * ITEMS + BASE)

                @block.tensor
                def _(pe):
                    def score_unit(n, i, t):
                        g, j = divmod(t, QUAD)
                        bank = s_bank0 + t % S_BANKS
                        s = slot(i)
                        pe.wait_ge(s_e, UNITS * n + t + 1 + BASE)
                        for k, q0, nq, off in S_UNITS[g]:
                            o = ps[:, bank, off * P:(off + nq) * P]
                            if latent:
                                for c in range(3):
                                    mm = nc.tensor.matmul(o, ks[0:97, s, c, k * P:(k + 1) * P],
                                                          qs[0:97, s, c, j, q0 * P:(q0 + nq) * P],
                                                          start=(c == 0), stop=(c == 2))
                            else:
                                mm = nc.tensor.matmul(o, qs[:, s, 1, j // 2, k * P:(k + 1) * P],
                                                      qs[:, s, 0, j, q0 * P:(q0 + nq) * P],
                                                      start=True, stop=True)
                        mm.then_inc(s_s, 1)

                    def max_unit(m, b, i, off, k):
                        j, g = divmod(k, ROWS_P)
                        n = m + off
                        s = slot(i, off)
                        if k == 0:
                            pe.wait_ge(s_ld[s], 16 * n_loads * uses(b, i, off) + BASE)
                        pe.wait_ge(s_mr, UNITS * n + k + 1 + BASE)
                        bank = m_bank0 + k % M_BANKS
                        for q, k0, nk, o_, _ in M_UNITS[g]:
                            o = ps[:, bank, o_ * P:(o_ + nk) * P]
                            has_diag = k0 + nk - 1 == q
                            if latent:
                                mm = nc.tensor.matmul(o, qs[0:96, s, 0, j, q * P:(q + 1) * P],
                                                      ks[0:96, s, 0, k0 * P:(k0 + nk) * P],
                                                      start=True, stop=not has_diag, skip_group_check=True)
                            else:
                                mm = nc.tensor.matmul(o, qs[:, s, 0, j, q * P:(q + 1) * P],
                                                      qs[:, s, 1, j // 2, k0 * P:(k0 + nk) * P],
                                                      start=True, stop=not has_diag, skip_group_check=True)
                            if has_diag:
                                mm = nc.tensor.matmul(ps[:, bank, (o_ + nk - 1) * P:(o_ + nk) * P],
                                                      ident_bf[:, :], causal_bf[:, :], start=False, stop=True,
                                                      skip_group_check=True)
                        mm.then_inc(s_m, 1)

                    def value_row(n, i, g):
                        s = slot(i)
                        pe.wait_ge(s_e, UNITS * n + QUAD * (g + 1) + S_BANKS + BASE)
                        if clip:
                            pe.wait_ge(s_clip, UNITS * n + QUAD * (g + 1) + BASE)
                        pe.wait_ge(s_sel, DIAGS * n + diags_before[g + 1] + BASE)
                        if g == 0:
                            pe.wait_ge(s_oc, n + BASE)
                        for k, q0, nq, off in S_UNITS[g]:
                            for bank, lo, hi in ((0, 0, 4), (1, 4, 8)):
                                a, z = max(q0, lo), min(q0 + nq, hi)
                                if a >= z:
                                    continue
                                for j in range(QUAD):
                                    v = vs[:, s, k, 0:VW] if latent else vs[:, s, k, j * VW:(j + 1) * VW]
                                    mm = nc.tensor.matmul(
                                        ps[VW * j:VW * (j + 1), o_bank + bank, (a - lo) * P:(z - lo) * P], v,
                                        pr_buf[:, (g % PRING) * QUAD + j, (off + a - q0) * P:(off + z - q0) * P],
                                        start=(k == 0), stop=(k == hi - 1), tile_position=(0, VW * j),
                                        skip_group_check=True)
                        mm.then_inc(s_pv, 1)

                    def first():
                        pe.sem_inc(s_pv, PRING)
                        if has_max:
                            if not latent:
                                pe.wait_ge(s_oneld[0], 16 * 4 + BASE)
                            for k in range(UNITS):
                                max_unit(0, 0, 0, 0, k)
                            for k in range(LEAD):
                                max_unit(0, 0, 0, 1, k)
                            if not latent:
                                pe.wait_ge(s_oneld[1], 16 * 4 + BASE)
                            else:
                                pe.wait_ge(s_one, 1 + BASE)

                    def item(b, i, last):
                        s = slot(i)
                        n = count_of(pe, b, i)
                        if has_max:
                            pe.wait_ge(s_mrow[s], 16 * (3 if latent else 2) * uses(b, i) + BASE)
                        pe.wait_ge(s_ld[s], 16 * n_loads * uses(b, i) + BASE)
                        for t in range(UNITS):
                            score_unit(n, i, t)
                            if has_max:
                                for off, k in m_events(t, last):
                                    max_unit(n, b, i, off, k)
                            if t == QUAD - 1 and last != 0:
                                value_row(n - 1, i - 1, ROWS_P - 1)
                            if t % QUAD == QUAD - 1 and t >= QUAD:
                                value_row(n, i, t // QUAD - 1)

                    run_items(pe, item, first, lambda: value_row(ITEMS - 1, ITEMS - 1, ROWS_P - 1))

                @block.scalar
                def _(act):
                    def item(b, i, last):
                        n = b * NQ + i
                        for t in range(UNITS):
                            g, j = divmod(t, QUAD)
                            act.wait_ge(s_s, UNITS * n + t + 1 + BASE)
                            if j == 0:
                                act.wait_ge(s_pv, ROWS_P * n + g + 1 + BASE)
                            nc.scalar.activation(pr_buf[:, (g % PRING) * QUAD + j, :],
                                                 ps[:, s_bank0 + t % S_BANKS, :], ACT.Exp, scale=scale)\
                                .then_inc(s_e, 1)

                    run_items(act, item, lambda: act.sem_inc(s_e, S_BANKS))

                @block.gpsimd
                def _(pool):
                    def item(b, i, last):
                        n = b * NQ + i
                        for t in range(UNITS):
                            g, j = divmod(t, QUAD)
                            for k, q0, nq, off in diag[g]:
                                if clip:
                                    wait_alone(pool, s_clip, UNITS * n + t + 1)
                                else:
                                    wait_alone(pool, s_e, UNITS * n + t + 1 + S_BANKS)
                                blk = pr_buf[:, (g % PRING) * QUAD + j, off * P:(off + 1) * P]
                                nc.gpsimd.affine_select(out=blk, in_=blk, compare_op=ALU.is_ge, fill=0.0, base=0,
                                                        pattern=[[1, P]], channel_multiplier=-1).then_inc(s_sel, 1)

                    if has_max and not latent:
                        nc.gpsimd.memset(minus_one, -1.0).then_inc(s_one, 1)
                    if not latent:
                        clear(pool, (2, 3), s_clear[1])
                    run_items(pool, item)

                @block.vector
                def _(dve):
                    def reduce_unit(m, i, off, k):
                        j, g = divmod(k, ROWS_P)
                        n = m + off
                        dve.wait_ge(s_m, UNITS * n + k + 1 + BASE)
                        if k == 0:
                            dve.wait_ge(s_pm, n + BASE)
                        bank = m_bank0 + k % M_BANKS
                        for q, k0, nk, o_, part in M_UNITS[g]:
                            r = nc.vector.tensor_reduce(pmax[:, j, q, part:part + 1],
                                                        ps[:, bank, o_ * P:(o_ + nk) * P], AX_X, ALU.max)
                        r.then_inc(s_mr, 1)
                        if k == UNITS - 1:
                            dve.wait_ge(s_mr, UNITS * (n + 1) + M_BANKS + BASE)
                            if not (isinstance(n, int) and n == 0):
                                dve.wait_ge(s_mT, n + BASE)
                            nc.vector.tensor_reduce(mx_sb[:, (i + off) % 2, :],
                                                    pmax[:, :, :, :].rearrange("p j q a -> p (j q) a"),
                                                    AX_X, ALU.max).then_inc(s_pm, 1)

                    def split_maxima(m, i, off):
                        n = m + off
                        mp = m_parts[:, (i + off) % 2, :, :]
                        dve.wait_ge(s_pm, n + 1 + BASE)
                        dve.wait_ge(s_m4, n + BASE)
                        nc.vector.transpose(mx_turned[:, :], mx_sb[:, (i + off) % 2, :]).then_inc(s_mT, 1)
                        dve.wait_ge(s_mT, n + 1 + BASE)
                        dve.wait_ge(s_mst, 16 * (P // MR) * n + BASE)
                        nc.vector.tensor_copy(mp[:, 0, :], mx_turned[:, :]).then_inc(s_m1, 1)
                        dve.wait_ge(s_m1, n + 1 + BASE)
                        nc.vector.tensor_tensor(m_rest[:, :], mx_turned[:, :], mp[:, 0, :], ALU.subtract)\
                            .then_inc(s_m2, 1)
                        dve.wait_ge(s_m2, n + 1 + BASE)
                        nc.vector.tensor_copy(mp[:, 1, :], m_rest[:, :]).then_inc(s_m3, 1)
                        dve.wait_ge(s_m3, n + 1 + BASE)
                        nc.vector.tensor_tensor(mp[:, 2, :], m_rest[:, :], mp[:, 1, :], ALU.subtract)\
                            .then_inc(s_m4, 1)

                    def first():
                        if not latent:
                            clear(dve, (0, 1), s_clear[0])
                        if has_max:
                            dve.sem_inc(s_mr, M_BANKS)
                            nc.vector.memset(pmax[:, :, :, :], -3.0e38).then_inc(s_pi, 1)
                            if latent:
                                nc.vector.memset(ks[96:97, :, :, :], -1.0).then_inc(s_one, 1)
                            dve.wait_ge(s_pi, 1 + BASE)
                            for k in range(UNITS):
                                reduce_unit(0, 0, 0, k)
                            split_maxima(0, 0, 0)
                            for k in range(LEAD):
                                reduce_unit(0, 0, 1, k)

                    def copy_outputs(n):
                        dve.wait_ge(s_pv, ROWS_P * (n + 1) + PRING + BASE)
                        dve.wait_ge(s_ost, 16 * n + BASE)
                        nc.vector.tensor_copy(o_sb[:, 0, :].rearrange("p (a t) -> p a t", a=2),
                                              ps[:, o_bank:o_bank + 2, :]).then_inc(s_oc, 1)

                    def item(b, i, last):
                        n = count_of(dve, b, i)
                        for t in range(UNITS):
                            g, j = divmod(t, QUAD)
                            if clip:
                                dve.wait_ge(s_e, UNITS * n + t + 1 + S_BANKS + BASE)
                                p = pr_buf[:, (g % PRING) * QUAD + j, :]
                                nc.vector.tensor_scalar(p, p, float(np.exp(-10.0)), float(np.exp(10.0)),
                                                        ALU.max, ALU.min).then_inc(s_clip, 1)
                            if has_max:
                                for off, k in m_events(t, last):
                                    reduce_unit(n, i, off, k)
                                if t == UNITS - LEAD + 1 and (last is None or last + 1 < ITEMS):
                                    split_maxima(n, i, 1)
                            if t == QUAD - 1 and last != 0:
                                copy_outputs(n - 1)

                    run_items(dve, item, first, lambda: copy_outputs(ITEMS - 1))

        def finish_heads8(name, wo):
            area_at[0] = 0
            norm = Norm(name + "ln")
            oT = work(2, NQ, CH)
            rden = work(2, CT, HEADS)
            on = work(2, CT, C)
            onT = work(2, CH)
            y = work(2, CT, C)
            s_ld = [sem(f"{name}_ld{u}") for u in range(2)]
            s_T = sem(name + "_T")
            s_rd = sem(name + "_rd")
            s_on = sem(name + "_on")
            s_T2 = sem(name + "_T2")
            s_c2 = sem(name + "_c2")
            s_y = sem(name + "_y")
            s_yc = sem(name + "_yc")
            s_res = sem(name + "_res")
            banks = (0, 1, 6, 7)
            with nc.Block() as block:
                @block.sync
                def _(sp):
                    def load(b, u, ahead):
                        sp.wait_ge(s_T, 8 * b + 4 * u + 1 + BASE)
                        sp.dma_start(oT[:, u, :, :],
                                     o_d[bass.ds(b * NQ, NQ), :, u * CH:(u + 1) * CH]
                                     .rearrange("n p t -> p n t")).then_inc(s_ld[u], 16)

                    run_chunks(sp, load)

                @block.tensor
                def _(pe):
                    pe.sem_inc(s_T, CT + 1)
                    if wo is not None:
                        pe.sem_inc(s_T2, 2)

                    def turn_outputs(b, u):
                        pe.wait_ge(s_ld[u], 16 * (b + 1) + BASE)
                        for t in range(CT):
                            pe.wait_ge(s_on, 8 * b + 4 * u + t + 1 + BASE)
                            for q in range(NQ):
                                i = nc.tensor.transpose(ps[:, banks[t], q * P:(q + 1) * P],
                                                        oT[:, u, q, t * P:(t + 1) * P], identity[:, :])
                            i.then_inc(s_T, 1)

                    def body(b, u, ahead):
                        if wo is not None:
                            pe.wait_ge(s_on, 8 * b + 4 * u + 4 + CT + BASE)
                            pe.wait_ge(s_c2, 2 * b + BASE)
                            transpose_chunk(2 + u, on[:, u, :, :]).then_inc(s_T2, 1)
                        if ahead is not None:
                            turn_outputs(*ahead)
                        if wo is not None:
                            pe.wait_ge(s_c2, 2 * b + u + 1 + BASE)
                            pe.wait_ge(s_yc, 2 * b + BASE)
                            for t in range(CT):
                                i = nc.tensor.matmul(ps[:, 4 + u, t * P:(t + 1) * P],
                                                     onT[:, u, t * P:(t + 1) * P], wo, start=True, stop=True)
                            i.then_inc(s_y, 1)

                    run_chunks(pe, body, (turn_outputs,))

                @block.scalar
                def _(act):
                    def body(b, u, ahead):
                        act.wait_ge(s_T2, 2 * b + u + 3 + BASE)
                        act.wait_ge(s_y, 2 * b + BASE)
                        nc.scalar.activation(onT[:, u, :], ps[:, 2 + u, :], ACT.Copy).then_inc(s_c2, 1)
                        act.wait_ge(s_y, 2 * b + u + 1 + BASE)
                        act.wait_ge(s_res, 2 * b + u + 1 + BASE)
                        nc.scalar.activation(y[:, u, :, :].rearrange("p a b -> p (a b)"), ps[:, 4 + u, :],
                                             ACT.Copy).then_inc(s_yc, 1)

                    if wo is not None:
                        run_chunks(act, body)

                @block.gpsimd
                def _(pool):
                    run_chunks(pool, lambda b, u, ahead: norm.inverse(pool, b, u))

                @block.vector
                def _(dve):
                    dve.sem_inc(s_on, CT)
                    dve.sem_inc(s_res, 2)

                    def normalise(b, u):
                        if wo is not None:
                            dve.wait_ge(s_T2, 2 * b + u + 1 + BASE)
                        for t in range(CT):
                            dve.wait_ge(s_T, 8 * b + 4 * u + t + 2 + CT + BASE)
                            o3 = ps[:, banks[t], :].rearrange("p (h w) -> p h w", w=VW)
                            nc.vector.reciprocal(rden[:, u, t, :], o3[:, :, 8]).then_inc(s_rd, 1)
                        for t in range(CT):
                            dve.wait_ge(s_rd, 8 * b + 4 * u + t + 1 + BASE)
                            o3 = ps[:, banks[t], :].rearrange("p (h w) -> p h w", w=VW)
                            nc.vector.tensor_tensor(
                                on[:, u, t, :].rearrange("p (h d) -> p h d", d=8), o3[:, :, 0:8],
                                rden[:, u, t, :].unsqueeze(2).to_broadcast([P, HEADS, 8]), ALU.mult)\
                                .then_inc(s_on, 1)

                    def statistics(b, u):
                        if wo is not None:
                            dve.wait_ge(s_yc, 2 * b + u + 1 + BASE)
                        else:
                            dve.wait_ge(s_on, 8 * b + 4 * u + 4 + CT + BASE)
                        norm.stats(dve, b, u, (y if wo is not None else on)[:, u, :, :])

                    def body(b, u, ahead):
                        if wo is None:
                            statistics(b, u)
                        if u == 1 and wo is None:
                            add(b, 0)
                        if ahead is not None:
                            normalise(*ahead)
                        if u == 1 and wo is not None:
                            add(b, 0)
                        if wo is not None:
                            statistics(b, u)

                    def add(b, u):
                        src = (y if wo is not None else on)[:, u, :, :]
                        norm.apply(dve, b, u, src, src)
                        dve.wait_ge(norm.s_out, 2 * b + u + 1 + BASE)
                        nc.vector.tensor_tensor(tiles_of(x_res, b, u), tiles_of(x_res, b, u), src, ALU.add)\
                            .then_inc(s_res, 1)

                    run_chunks(dve, body, (normalise,), lambda b: add(b, 1))

        def project_latent():
            name = "pl"
            area_at[0] = 0
            norm = Norm(name + "ln")
            rms = RootMean(name + "rm")
            xr = work(2, CT, C)
            xrT = work(2, CH)
            JOBS = 7
            t_cos = work(2, CH)
            t_sin = work(2, CH)
            val = work(JOBS, CH)
            rest = work(JOBS, CH)
            parts = work(JOBS, 3, CH, dt=BF16)
            v_pad = work(2, CT, VW)
            xx = work(2, CT, C)
            table = {n: work(T, parts=consts[n].shape[0]) for n in TABLES}
            s_tab = sem(name + "_tab")
            s_xst = [sem(f"{name}_xst{u}") for u in range(2)]
            s_pad = sem(name + "_pad")
            s_T = sem(name + "_T")
            s_xT = sem(name + "_xT")
            s_v = sem(name + "_v")
            s_vp = sem(name + "_vp")
            s_vst = [sem(f"{name}_vst{u}") for u in range(2)]
            s_mm = sem(name + "_mm")
            s_cs = sem(name + "_cs")
            s_val = sem(name + "_val")
            s_p1 = sem(name + "_p1")
            s_r1 = sem(name + "_r1")
            s_p2 = sem(name + "_p2")
            s_p3 = sem(name + "_p3")
            s_st = [sem(f"{name}_st{j}") for j in range(JOBS)]
            tab = {True: ("cos_k", "sin_k"), False: ("cos_q", "sin_q")}

            def job(b, u, j):
                return b * 2 * JOBS + u * JOBS + j, (u * JOBS + j) % 2, (MD if j == 6 else P), j not in (4, 5)

            def stores(j):
                return 6 if j == JOBS - 1 else 3

            def behind(u, j, d):
                at = u * JOBS + j - d
                return divmod(at, JOBS) if 0 <= at < 2 * JOBS else None

            def step_ahead(j, ahead, at):
                if ahead is not None and j in at:
                    at[j](*ahead)

            with nc.Block() as block:
                @block.vector
                def _(dve):
                    nc.vector.memset(v_pad, 0.0).then_inc(s_pad, 1)
                    dve.wait_ge(s_pad, 1 + BASE)
                    nc.vector.memset(v_pad[:, :, :, LAT:LAT + 1], 1.0).then_inc(s_pad, 1)
                    dve.sem_inc(s_cs, 2)
                    dve.wait_ge(s_tab, 16 * len(TABLES) + BASE)

                    def statistics(b, u):
                        norm.stats(dve, b, u, tiles_of(x_res, b, u))

                    def apply(b, u):
                        dve.wait_ge(rms.s_out, 2 * b + BASE)
                        dve.wait_ge(s_xst[u], 16 * b + BASE)
                        norm.apply(dve, b, u, tiles_of(x_res, b, u), xx[:, u, :, :])

                    def third_part(b, u, j):
                        n, r, rows, rot = job(b, u, j)
                        dve.wait_ge(s_p2, n + 1 + BASE)
                        nc.vector.tensor_tensor(parts[0:rows, j, 2, :], rest[0:rows, j, :],
                                                parts[0:rows, j, 1, :], ALU.subtract).then_inc(s_p3, 1)

                    def jobs(b, u, ahead):
                        dve.wait_ge(s_v, 2 * b + u + 1 + BASE)
                        dve.wait_ge(s_vst[u], 16 * b + BASE)
                        nc.vector.tensor_copy(v_pad[:, u, :, 0:LAT],
                                              ps[:, 2 + u, 0:CT * LAT].rearrange("p (t r) -> p t r", t=CT))\
                            .then_inc(s_vp, 1)
                        for j in range(JOBS):
                            n, r, rows, rot = job(b, u, j)
                            dve.wait_ge(s_mm, n + 1 + JOBS + BASE)
                            if rot:
                                dve.wait_ge(s_val, n + BASE)
                                cs, sn = tab[j == 6]
                                nc.vector.tensor_tensor(t_cos[0:rows, r, :], ps[0:rows, 4 + 2 * r, :],
                                                        table[cs][:, u * CH:(u + 1) * CH], ALU.mult)
                                nc.vector.tensor_tensor(t_sin[0:rows, r, :], ps[0:rows, 5 + 2 * r, :],
                                                        table[sn][:, u * CH:(u + 1) * CH], ALU.mult)\
                                    .then_inc(s_cs, 1)
                            else:
                                dve.wait_ge(s_r1, n + 1 + BASE)
                                nc.vector.tensor_copy(val[:, j, :], ps[:, 4 + 2 * r, :]).then_inc(s_cs, 1)
                            old = behind(u, j, 3)
                            if old is not None:
                                third_part(b, *old)
                            step_ahead(j, ahead, {0: statistics, 1: apply})

                    def drain(b):
                        for d in (3, 2, 1):
                            third_part(b, 1, JOBS - d)

                    run_chunks(dve, jobs, (statistics, apply), drain)

                @block.gpsimd
                def _(pool):
                    pool.sem_inc(rms.s_go, 1)
                    pool.sem_inc(s_val, 1)
                    pool.sem_inc(s_r1, JOBS)

                    def first_rest(b, u, j):
                        n, r, rows, rot = job(b, u, j)
                        pool.wait_ge(s_p1, n + 1 + BASE)
                        pool.wait_ge(s_p3, n + 1 + BASE)
                        nc.gpsimd.tensor_tensor(rest[0:rows, j, :], val[0:rows, j, :],
                                                parts[0:rows, j, 0, :], ALU.subtract).then_inc(s_r1, 1)

                    def jobs(b, u, ahead):
                        for j in range(JOBS):
                            n, r, rows, rot = job(b, u, j)
                            if rot:
                                wait_alone(pool, s_cs, n + 1 + 2, (s_r1, n + 1))
                                nc.gpsimd.tensor_tensor(val[0:rows, j, :], t_cos[0:rows, r, :],
                                                        t_sin[0:rows, r, :], ALU.add).then_inc(s_val, 1)
                            else:
                                pool.wait_ge(s_cs, n + 1 + 2 + BASE)
                                pool.wait_ge(s_val, n + 1 + BASE)
                                pool.sem_inc(s_val, 1)
                            old = behind(u, j, 1)
                            if old is not None:
                                first_rest(b, *old)
                            step_ahead(j, ahead, {0: lambda b, u: norm.inverse(pool, b, u),
                                                  2: lambda b, u: rms.inverse(pool, b, u)})

                    run_chunks(pool, jobs, (lambda b, u: norm.inverse(pool, b, u),
                                            lambda b, u: rms.inverse(pool, b, u)),
                               lambda b: first_rest(b, 1, JOBS - 1))

                @block.tensor
                def _(pe):
                    pe.sem_inc(s_mm, JOBS)

                    def turn(b, u):
                        pe.wait_ge(rms.s_out, 2 * b + u + 1 + BASE)
                        pe.wait_ge(s_xT, 2 * b + BASE)
                        transpose_chunk(u, xr[:, u, :, :]).then_inc(s_T, 1)

                    def jobs(b, u, ahead):
                        pe.wait_ge(s_xT, 2 * b + u + 1 + BASE)
                        pe.wait_ge(s_vp, 2 * b + BASE)
                        for t in range(CT):
                            i = nc.tensor.matmul(ps[:, 2 + u, t * LAT:(t + 1) * LAT],
                                                 xrT[:, u, t * P:(t + 1) * P], w_sb["wkva"][:, 0:LAT],
                                                 start=True, stop=True)
                        i.then_inc(s_v, 1)
                        for j in range(JOBS):
                            n, r, rows, rot = job(b, u, j)
                            pe.wait_ge(s_cs, n + 1 + BASE)
                            if j < 4:
                                wa, wb = w_sb["wq_rope"][:, j, :], w_sb["wq_rope_sw"][:, j, :]
                            elif j < 6:
                                wa = wabs[:, j - 4, :, :, :].rearrange("p a b c -> p (a b c)")
                            else:
                                wa, wb = w_sb["wkva"][:, :], w_sb["wkva_sw"][:, :]
                            i = nc.tensor.matmul(ps[0:rows, 4 + 2 * r, :], wa, xrT[:, u, :], start=True, stop=True)
                            if rot:
                                i = nc.tensor.matmul(ps[0:rows, 5 + 2 * r, :], wb, xrT[:, u, :],
                                                     start=True, stop=True)
                            i.then_inc(s_mm, 1)
                            step_ahead(j, ahead, {5: turn})

                    run_chunks(pe, jobs, (turn,))

                @block.scalar
                def _(act):
                    def squares(b, u):
                        act.wait_ge(norm.s_out, 2 * b + u + 1 + BASE)
                        rms.squares(act, b, u, xx[:, u, :, :])

                    def apply(b, u):
                        rms.apply(act, b, u, xx[:, u, :, :], xr[:, u, :, :], (s_T, 2 * b))

                    def copy_turned(b, u):
                        act.wait_ge(s_T, 2 * b + u + 1 + BASE)
                        act.wait_ge(s_mm, JOBS * (2 * b + u) + BASE)
                        nc.scalar.activation(xrT[:, u, :], ps[:, u, :], ACT.Copy, scale=w_sb["ln1"][:, 0:1])\
                            .then_inc(s_xT, 1)

                    def second_part(b, u, j):
                        n, r, rows, rot = job(b, u, j)
                        act.wait_ge(s_r1, n + 1 + JOBS + BASE)
                        nc.scalar.activation(parts[0:rows, j, 1, :], rest[0:rows, j, :], ACT.Copy)\
                            .then_inc(s_p2, 1)

                    def jobs(b, u, ahead):
                        for j in range(JOBS):
                            n, r, rows, rot = job(b, u, j)
                            act.wait_ge(s_val, n + 2 + BASE)
                            act.wait_ge(s_st[j], 16 * stores(j) * (2 * b + u) + BASE)
                            nc.scalar.activation(parts[0:rows, j, 0, :], val[0:rows, j, :], ACT.Copy)\
                                .then_inc(s_p1, 1)
                            old = behind(u, j, 1)
                            if old is not None:
                                second_part(b, *old)
                            step_ahead(j, ahead, {1: squares, 3: apply, 5: copy_turned})

                    run_chunks(act, jobs, (squares, apply, copy_turned), lambda b: second_part(b, 1, JOBS - 1))

                @block.sync
                def _(sp):
                    sp.wait_ge(s_pad, 2 + BASE)
                    sp.sem_inc(s_p3, JOBS)
                    for n in TABLES:
                        sp.dma_start(table[n], consts[n]).then_inc(s_tab, 16)

                    def store_xx(b, u):
                        sp.wait_ge(norm.s_out, 2 * b + u + 1 + BASE)
                        sp.dma_start(xx_d[bass.ds(b * T + u * CH, CH), :].rearrange("(t p) c -> p t c", p=P),
                                     xx[:, u, :, :]).then_inc(s_xst[u], 16)

                    def jobs(b, u, ahead):
                        sp.wait_ge(s_vp, 2 * b + u + 1 + BASE)
                        sp.dma_start(vm_d[bass.ds(b * T + u * CH, CH), :].rearrange("(t p) w -> p t w", p=P),
                                     v_pad[:, u, :, :]).then_inc(s_vst[u], 16)
                        tok = slice(u * CH, (u + 1) * CH)
                        for j in range(JOBS):
                            n, r, rows, rot = job(b, u, j)
                            wait_alone(sp, s_p3, n + 1 + JOBS)
                            if j < 4:
                                for part in range(3):
                                    sp.dma_start(qm_d[bass.ds(b * NQ + j, 1), part, LAT:MD, :, tok]
                                                 .rearrange("n r h t -> (n r h) t"),
                                                 parts[:, j, part, :]).then_inc(s_st[j], 16)
                            elif j < 6:
                                for part in range(3):
                                    sp.dma_start(qm_d[bass.ds(b * NQ + 2 * (j - 4), 2), part, 0:LAT, :, tok]
                                                 .rearrange("n r h t -> n (r h) t"),
                                                 parts[:, j, part, :]).then_inc(s_st[j], 16)
                            else:
                                for t in range(6):
                                    sp.dma_start(kterm_d[t // 2][bass.ds(b, 1), (t % 2) * MD:(t % 2 + 1) * MD, tok]
                                                 .rearrange("n r t -> (n r) t"),
                                                 parts[0:MD, j, KTERM[t], :]).then_inc(s_st[j], 16)
                            step_ahead(j, ahead, {0: store_xx})

                    run_chunks(sp, jobs, (store_xx,))
                    for u in range(2):
                        sp.wait_ge(s_vst[u], 16 * BATCH + BASE)
                        sp.wait_ge(s_xst[u], 16 * BATCH + BASE)
                    for j in range(JOBS):
                        sp.wait_ge(s_st[j], 16 * stores(j) * 2 * BATCH + BASE)

        x2_res = v_buf[:, :, :].rearrange("p a b -> p (a b)").rearrange("p (t c) -> p t c", c=C)

        def finish_latent():
            name = "fl"
            area_at[0] = 0
            oT = work(2, NQ, CH)
            rden = work(2, CT, HEADS)
            on = work(2, CT, 2 * P)
            onT = work(2, 2, CH)
            xx = work(2, CT, C)
            s_xx = [sem(f"{name}_xx{u}") for u in range(2)]
            s_ld = [sem(f"{name}_ld{u}") for u in range(2)]
            s_T = sem(name + "_T")
            s_rd = sem(name + "_rd")
            s_on = sem(name + "_on")
            s_T2 = sem(name + "_T2")
            s_c2 = sem(name + "_c2")
            s_y = sem(name + "_y")
            s_x2 = sem(name + "_x2")
            with nc.Block() as block:
                @block.sync
                def _(sp):
                    def load(b, u, ahead):
                        sp.wait_ge(s_T, 8 * b + 4 * u + 1 + BASE)
                        sp.dma_start(oT[:, u, :, :],
                                     o_d[bass.ds(b * NQ, NQ), :, u * CH:(u + 1) * CH]
                                     .rearrange("n p t -> p n t")).then_inc(s_ld[u], 16)
                        sp.wait_ge(s_x2, 2 * b + u + 1 + BASE)
                        sp.dma_start(xx[:, u, :, :],
                                     xx_d[bass.ds(b * T + u * CH, CH), :].rearrange("(t p) c -> p t c", p=P))\
                            .then_inc(s_xx[u], 16)

                    run_chunks(sp, load)

                @block.tensor
                def _(pe):
                    pe.sem_inc(s_T, CT + 1)
                    pe.sem_inc(s_T2, 3)

                    def turn_outputs(b, u):
                        pe.wait_ge(s_ld[u], 16 * (b + 1) + BASE)
                        for t in range(CT):
                            pe.wait_ge(s_on, 8 * b + 4 * u + t + 1 + BASE)
                            for q in range(NQ):
                                i = nc.tensor.transpose(ps[:, t % 2, q * P:(q + 1) * P],
                                                        oT[:, u, q, t * P:(t + 1) * P], identity[:, :])
                            i.then_inc(s_T, 1)

                    def body(b, u, ahead):
                        pe.wait_ge(s_on, 8 * b + 4 * u + 4 + 2 + BASE)
                        pe.wait_ge(s_c2, 4 * b + BASE)
                        for half in range(2):
                            for t in range(CT):
                                i = nc.tensor.transpose(ps[:, 2 + 2 * u + half, t * P:(t + 1) * P],
                                                        on[:, u, t, half * P:(half + 1) * P], identity[:, :])
                            i.then_inc(s_T2, 1)
                        if ahead is not None:
                            turn_outputs(*ahead)
                        pe.wait_ge(s_c2, 4 * b + 2 * u + 2 + BASE)
                        pe.wait_ge(s_x2, 2 * b + u + 1 + BASE)
                        for t in range(CT):
                            for half in range(2):
                                i = nc.tensor.matmul(ps[:, 6 + u, t * P:(t + 1) * P],
                                                     onT[:, u, half, t * P:(t + 1) * P], wout_m[:, half, :],
                                                     start=(half == 0), stop=(half == 1))
                        i.then_inc(s_y, 1)

                    run_chunks(pe, body, (turn_outputs,))

                @block.scalar
                def _(act):
                    def body(b, u, ahead):
                        for half in range(2):
                            act.wait_ge(s_T2, 4 * b + 2 * u + half + 4 + BASE)
                            act.wait_ge(s_y, 2 * b + BASE)
                            nc.scalar.activation(onT[:, u, half, :], ps[:, 2 + 2 * u + half, :], ACT.Copy)\
                                .then_inc(s_c2, 1)

                    run_chunks(act, body)

                @block.vector
                def _(dve):
                    dve.sem_inc(s_on, 2)
                    dve.sem_inc(s_x2, 2)

                    def normalise(b, u):
                        dve.wait_ge(s_T2, 4 * b + 2 * u + 1 + BASE)
                        for t in range(CT):
                            dve.wait_ge(s_T, 8 * b + 4 * u + t + 2 + CT + BASE)
                            o3 = ps[:, t % 2, :].rearrange("p (h w) -> p h w", w=VW)
                            nc.vector.reciprocal(rden[:, u, t, :], o3[:, :, LAT]).then_inc(s_rd, 1)
                            dve.wait_ge(s_rd, 8 * b + 4 * u + t + 1 + BASE)
                            nc.vector.tensor_tensor(
                                on[:, u, t, :].rearrange("p (h d) -> p h d", d=LAT), o3[:, :, 0:LAT],
                                rden[:, u, t, :].unsqueeze(2).to_broadcast([P, HEADS, LAT]), ALU.mult)\
                                .then_inc(s_on, 1)

                    def body(b, u, ahead):
                        if ahead is not None:
                            normalise(*ahead)
                        dve.wait_ge(s_y, 2 * b + u + 1 + BASE)
                        dve.wait_ge(s_xx[u], 16 * (b + 1) + BASE)
                        nc.vector.tensor_tensor(
                            tiles_of(x2_res, b, u), ps[:, 6 + u, :].rearrange("p (t c) -> p t c", c=C),
                            xx[:, u, :, :], ALU.add).then_inc(s_x2, 1)

                    run_chunks(dve, body, (normalise,))

        def experts():
            name = "me"
            area_at[0] = 0
            norm = Norm(name + "ln")
            rms = RootMean(name + "rm")
            GP = PAIRS + 1
            xr = work(2, CT, C)
            xrT = work(2, CH)
            prob = work(2, CT, EXPERTS)
            red = work(2, CT)
            cmp1 = work(2, CT, EXPERTS, EXPERTS)
            cmp2 = work(2, CT, EXPERTS, EXPERTS)
            rank = work(2, CT, EXPERTS)
            comb = work(2, CT, EXPERTS)
            combT = work(2, CH)
            silu = work(2, CH)
            hT = work(2, GP, CH)
            ffn = work(2, CT, C)
            s_T = sem(name + "_T")
            s_xT = sem(name + "_xT")
            s_lg = sem(name + "_lg")
            s_g = sem(name + "_g")
            s_gs = sem(name + "_gs")
            s_ex = sem(name + "_ex")
            s_cT = sem(name + "_cT")
            s_cc = sem(name + "_cc")
            s_gu = sem(name + "_gu")
            s_cb = sem(name + "_cb")
            s_si = sem(name + "_si")
            s_h = sem(name + "_h")
            s_hc = sem(name + "_hc")
            s_z = sem(name + "_z")
            s_ff = sem(name + "_ff")
            s_res = sem(name + "_res")
            GATE = 12

            def run_sequences(eng, body, front):
                front(0)
                with eng.Fori(0, BATCH - 1) as b:
                    body(b, b + 1)
                body(BATCH - 1, None)

            with nc.Block() as block:
                @block.scalar
                def _(act):
                    def squares(b, u):
                        rms.squares(act, b, u, tiles_of(x2_res, b, u))

                    def apply(b, u):
                        rms.apply(act, b, u, tiles_of(x2_res, b, u), xr[:, u, :, :], (s_T, 2 * b))

                    def rest_of_front(b):
                        for u in range(2):
                            act.wait_ge(s_T, 2 * b + u + 1 + BASE)
                            act.wait_ge(s_gu, 2 * GP * b + BASE)
                            nc.scalar.activation(xrT[:, u, :], ps[:, 0, :], ACT.Copy, scale=w_sb["ln2"][:, 0:1])\
                                .then_inc(s_xT, 1)
                        for u in range(2):
                            act.wait_ge(s_g, GATE * (2 * b + u) + 3 + BASE)
                            nc.scalar.activation(prob[:, u, :, :], prob[:, u, :, :], ACT.Exp).then_inc(s_ex, 1)
                        for u in range(2):
                            act.wait_ge(s_cT, 2 * b + u + 1 + BASE)
                            nc.scalar.activation(combT[0:EXPERTS, u, :], ps[0:EXPERTS, 1, :], ACT.Copy)\
                                .then_inc(s_cc, 1)

                    def front(b):
                        for step in (squares, apply):
                            for u in range(2):
                                step(b, u)
                        rest_of_front(b)

                    def body(b, following):
                        steps = {1: (squares, 0), 2: (squares, 1), GP: (apply, 0), GP + 2: (apply, 1)}
                        for u in range(2):
                            for j in range(GP):
                                n = 2 * GP * b + GP * u + j
                                rows = P if j < PAIRS else INNER
                                act.wait_ge(s_gu, n + 1 + BASE)
                                act.wait_ge(s_h, n + 1 + BASE)
                                nc.scalar.activation(silu[0:rows, (GP * u + j) % 2, :],
                                                     ps[0:rows, 2 + (GP * u + j) % 2, :], ACT.Silu).then_inc(s_si, 1)
                                if following is not None and GP * u + j in steps:
                                    step, half = steps[GP * u + j]
                                    step(following, half)
                        if following is not None:
                            rest_of_front(following)

                    run_sequences(act, body, front)

                @block.gpsimd
                def _(pool):
                    pool.sem_inc(rms.s_go, 1)

                    def front(b):
                        for u in range(2):
                            rms.inverse(pool, b, u)

                    def body(b, following):
                        if following is not None:
                            front(following)
                        for u in range(2):
                            norm.inverse(pool, b, u)

                    run_sequences(pool, body, front)

                @block.tensor
                def _(pe):
                    def logits(b):
                        pe.wait_ge(s_hc, 2 * PAIRS * b + BASE)
                        for u in range(2):
                            pe.wait_ge(rms.s_out, 2 * b + u + 1 + BASE)
                            pe.wait_ge(s_xT, 2 * b + u + BASE)
                            transpose_chunk(0, xr[:, u, :, :]).then_inc(s_T, 1)
                        for u in range(2):
                            pe.wait_ge(s_xT, 2 * b + u + 1 + BASE)
                            pe.wait_ge(s_cc, 2 * b + BASE)
                            for t in range(CT):
                                i = nc.tensor.matmul(ps[:, 1, (u * CT + t) * EXPERTS:(u * CT + t + 1) * EXPERTS],
                                                     xrT[:, u, t * P:(t + 1) * P], w_sb["wgate"][:, :],
                                                     start=True, stop=True)
                            i.then_inc(s_lg, 1)

                    def turn_gates(b):
                        pe.wait_ge(s_g, GATE * (2 * b + 2) + BASE)
                        for u in range(2):
                            pe.wait_ge(s_cc, 2 * b + u + BASE)
                            for t in range(CT):
                                i = nc.tensor.transpose(ps[0:EXPERTS, 1, t * P:(t + 1) * P], comb[:, u, t, :],
                                                        identity[:, :])
                            i.then_inc(s_cT, 1)

                    def front(b):
                        logits(b)
                        turn_gates(b)

                    def body(b, following):
                        for u in range(2):
                            pe.wait_ge(s_cc, 2 * b + u + 1 + BASE)
                            for j in range(GP):
                                n = 2 * GP * b + GP * u + j
                                rows = P if j < PAIRS else INNER
                                r = (GP * u + j) % 2
                                pe.wait_ge(s_h, n + 1 + BASE)
                                nc.tensor.matmul(ps[0:rows, 2 + r, :], w_sb["wg"][:, j * P:j * P + rows],
                                                 xrT[:, u, :], start=True, stop=True)
                                nc.tensor.matmul(ps[0:rows, 4 + r, :], w_sb["wu"][:, j * P:j * P + rows],
                                                 xrT[:, u, :], start=True, stop=True).then_inc(s_gu, 1)
                                if j < PAIRS:
                                    pe.wait_ge(s_hc, PAIRS * (2 * b + u) + j + BASE)
                                    nc.tensor.matmul(ps[:, 0, :], w_sb["spread"][:, j * P:(j + 1) * P],
                                                     combT[0:EXPERTS, u, :], start=True, stop=True).then_inc(s_cb, 1)
                        if following is not None:
                            logits(following)
                        for u in range(2):
                            pe.wait_ge(s_hc, PAIRS * (2 * b + u + 1) + BASE)
                            pe.wait_ge(s_h, GP * (2 * b + u + 1) + 2 + BASE)
                            pe.wait_ge(s_ff, 2 * b + BASE)
                            for t in range(CT):
                                for j in range(GP):
                                    rows = P if j < PAIRS else INNER
                                    i = nc.tensor.matmul(ps[:, 6 + u, t * P:(t + 1) * P],
                                                         hT[0:rows, u, j, t * P:(t + 1) * P],
                                                         w_sb["wd"][0:rows, j, :], start=(j == 0), stop=(j == GP - 1))
                            i.then_inc(s_z, 1)
                        if following is not None:
                            turn_gates(following)

                    run_sequences(pe, body, front)

                @block.vector
                def _(dve):
                    dve.sem_inc(s_h, 2)

                    def gate(b, u):
                        c = [GATE * (2 * b + u)]

                        def step(i):
                            i.then_inc(s_g, 1)
                            c[0] = c[0] + 1
                            dve.wait_ge(s_g, c[0] + BASE)

                        pr = prob[:, u, :, :]
                        shape = [P, CT, EXPERTS]
                        big = [P, CT, EXPERTS, EXPERTS]
                        dve.wait_ge(s_lg, 2 * b + 2 + BASE)
                        step(nc.vector.tensor_tensor(
                            pr, ps[:, 1, u * CT * EXPERTS:(u + 1) * CT * EXPERTS].rearrange("p (t e) -> p t e", t=CT),
                            w_sb["bias"][:, :].unsqueeze(1).to_broadcast(shape), ALU.add))
                        step(nc.vector.tensor_reduce(red[:, u, :], pr, AX_X, ALU.max))
                        nc.vector.tensor_tensor(pr, pr, red[:, u, :].unsqueeze(2).to_broadcast(shape), ALU.subtract)\
                            .then_inc(s_g, 1)
                        c[0] = c[0] + 1
                        dve.wait_ge(s_ex, 2 * b + u + 1 + BASE)
                        step(nc.vector.tensor_reduce(red[:, u, :], pr, AX_X, ALU.add))
                        step(nc.vector.reciprocal(red[:, u, :], red[:, u, :]))
                        step(nc.vector.tensor_tensor(pr, pr, red[:, u, :].unsqueeze(2).to_broadcast(shape), ALU.mult))
                        other = pr.unsqueeze(2).to_broadcast(big)
                        own = pr.unsqueeze(3).to_broadcast(big)
                        nc.vector.tensor_tensor(cmp1[:, u, :, :, :], other, own, ALU.is_gt)
                        step(nc.vector.tensor_tensor(cmp2[:, u, :, :, :], other, own, ALU.is_equal))
                        step(nc.vector.tensor_tensor(
                            cmp2[:, u, :, :, :], cmp2[:, u, :, :, :],
                            w_sb["earlier"][:, :].rearrange("p (a b) -> p a b", a=EXPERTS)
                            .unsqueeze(1).to_broadcast(big), ALU.mult))
                        step(nc.vector.tensor_tensor(cmp1[:, u, :, :, :], cmp1[:, u, :, :, :], cmp2[:, u, :, :, :],
                                                     ALU.add))
                        step(nc.vector.tensor_reduce(rank[:, u, :, :], cmp1[:, u, :, :, :], AX_X, ALU.add))
                        step(nc.vector.scalar_tensor_tensor(out=comb[:, u, :, :], in0=rank[:, u, :, :],
                                                            scalar=TOPK - 0.5, in1=pr, op0=ALU.is_lt, op1=ALU.mult))
                        nc.vector.tensor_reduce(red[:, u, :], comb[:, u, :, :], AX_X, ALU.add).then_inc(s_gs, 1)
                        dve.wait_ge(s_gs, 2 * (2 * b + u) + 1 + BASE)
                        nc.vector.reciprocal(red[:, u, :], red[:, u, :]).then_inc(s_gs, 1)
                        dve.wait_ge(s_gs, 2 * (2 * b + u) + 2 + BASE)
                        nc.vector.tensor_tensor(comb[:, u, :, :], comb[:, u, :, :],
                                                red[:, u, :].unsqueeze(2).to_broadcast(shape), ALU.mult)\
                            .then_inc(s_g, 1)

                    def front(b):
                        for u in range(2):
                            dve.wait_ge(s_cT, 2 * b + BASE)
                            gate(b, u)

                    def body(b, following):
                        for u in range(2):
                            dve.wait_ge(s_z, 2 * b + BASE)
                            for j in range(GP):
                                n = 2 * GP * b + GP * u + j
                                rows = P if j < PAIRS else INNER
                                r = (GP * u + j) % 2
                                dve.wait_ge(s_si, n + 1 + BASE)
                                nc.vector.tensor_tensor(hT[0:rows, u, j, :], ps[0:rows, 4 + r, :],
                                                        silu[0:rows, r, :], ALU.mult).then_inc(s_h, 1)
                                if j < PAIRS:
                                    dve.wait_ge(s_h, n + 1 + 2 + BASE)
                                    dve.wait_ge(s_cb, PAIRS * (2 * b + u) + j + 1 + BASE)
                                    nc.vector.tensor_tensor(hT[:, u, j, :], ps[:, 0, :], hT[:, u, j, :], ALU.mult)\
                                        .then_inc(s_hc, 1)
                        if following is not None:
                            front(following)
                        for u in range(2):
                            dve.wait_ge(s_z, 2 * b + u + 1 + BASE)
                            dve.wait_ge(s_res, 2 * b + BASE)
                            nc.vector.tensor_tensor(ffn[:, u, :, :],
                                                    ps[:, 6 + u, :].rearrange("p (t c) -> p t c", c=C),
                                                    tiles_of(x2_res, b, u), ALU.add).then_inc(s_ff, 1)
                            dve.wait_ge(s_ff, 2 * b + u + 1 + BASE)
                            norm.stats(dve, b, u, ffn[:, u, :, :])
                        for u in range(2):
                            norm.apply(dve, b, u, ffn[:, u, :, :], ffn[:, u, :, :])
                            dve.wait_ge(norm.s_out, 2 * b + u + 1 + BASE)
                            nc.vector.tensor_tensor(tiles_of(x_res, b, u), tiles_of(x_res, b, u), ffn[:, u, :, :],
                                                    ALU.add).then_inc(s_res, 1)

                    run_sequences(dve, body, front)

        def low_rank_ffn():
            name = "lf"
            area_at[0] = 0
            norm = Norm(name + "a")
            norm2 = Norm(name + "b")
            FB = DFF // P
            w1 = work(DFF)
            w2 = work(FB, C)
            xn = work(2, CT, C)
            xnT = work(2, CH)
            hT = work(2, FB, CH)
            y = work(2, CT, C)
            h_bank0, y_bank0 = 2, 6
            s_T = sem(name + "_T")
            s_xT = sem(name + "_xT")
            s_h = sem(name + "_h")
            s_gl = sem(name + "_gl")
            s_y = sem(name + "_y")
            s_yb = sem(name + "_yb")
            s_res = sem(name + "_res")
            s_st = [sem(f"{name}_st{u}") for u in range(2)]
            s_fold = sem(name + "_fold")
            s_w = sem(name + "_w")
            with nc.Block() as block:
                @block.vector
                def _(dve):
                    dve.sem_inc(s_yb, 2)
                    dve.wait_ge(s_fold, 1 + BASE)
                    nc.vector.tensor_copy(w1, ps[:, h_bank0, :])
                    nc.vector.tensor_copy(w2.rearrange("p f c -> p (f c)"), ps[:, h_bank0 + 1, :]).then_inc(s_w, 1)

                    def front(b, u):
                        norm.stats(dve, b, u, tiles_of(x_res, b, u))
                        dve.wait_ge(s_T, 2 * b + BASE)
                        norm.apply(dve, b, u, tiles_of(x_res, b, u), xn[:, u, :, :])

                    def body(b, u, ahead):
                        if not isinstance(b, int):
                            front(b + 1, u)
                        dve.wait_ge(s_y, 2 * b + u + 3 + BASE)
                        dve.wait_ge(s_res, 2 * b + BASE)
                        nc.vector.tensor_tensor(y[:, u, :, :],
                                                ps[:, y_bank0 + u, :].rearrange("p (t c) -> p t c", c=C),
                                                w_sb["b2"][:, :].unsqueeze(1).to_broadcast([P, CT, C]), ALU.add)\
                            .then_inc(s_yb, 1)
                        dve.wait_ge(s_yb, 2 * b + u + 3 + BASE)
                        norm2.stats(dve, b, u, y[:, u, :, :])
                        norm2.apply(dve, b, u, y[:, u, :, :], y[:, u, :, :])
                        dve.wait_ge(norm2.s_out, 2 * b + u + 1 + BASE)
                        nc.vector.tensor_tensor(tiles_of(x_res, b, u), tiles_of(x_res, b, u), y[:, u, :, :],
                                                ALU.add).then_inc(s_res, 1)

                    run_chunks(dve, body, (front, lambda b, u: front(0, 1)))

                @block.gpsimd
                def _(pool):
                    def body(b, u, ahead):
                        if not isinstance(b, int):
                            norm.inverse(pool, b + 1, u)
                        norm2.inverse(pool, b, u)

                    run_chunks(pool, body, (lambda b, u: norm.inverse(pool, 0, 0),
                                            lambda b, u: norm.inverse(pool, 0, 1)))

                @block.tensor
                def _(pe):
                    pe.sem_inc(s_h, FB + 1)
                    pe.sem_inc(s_y, 2)
                    nc.tensor.matmul(ps[:, h_bank0, :], w_sb["u1t"][:, :], w_sb["v1"][:, :], start=True, stop=True)
                    for f in range(FB):
                        i = nc.tensor.matmul(ps[:, h_bank0 + 1, f * C:(f + 1) * C], w_sb["u2t"][:, f * P:(f + 1) * P],
                                             w_sb["v2"][:, :], start=True, stop=True)
                    i.then_inc(s_fold, 1)

                    def turn(b, u):
                        pe.wait_ge(norm.s_out, 2 * b + u + 1 + BASE)
                        pe.wait_ge(s_xT, 2 * b + BASE)
                        transpose_chunk(u, xn[:, u, :, :]).then_inc(s_T, 1)

                    def body(b, u, ahead):
                        pe.wait_ge(s_xT, 2 * b + u + 1 + BASE)
                        for f in range(FB):
                            pe.wait_ge(s_gl, FB * (2 * b + u) + f + 1 + BASE)
                            nc.tensor.matmul(ps[:, h_bank0 + f, :], w1[:, f * P:(f + 1) * P], xnT[:, u, :],
                                             start=True, stop=True).then_inc(s_h, 1)
                        if ahead is not None:
                            turn(*ahead)
                        pe.wait_ge(s_yb, 2 * b + u + 1 + BASE)
                        pe.wait_ge(s_gl, FB * (2 * b + u + 2) + BASE)
                        for t in range(CT):
                            for f in range(FB):
                                i = nc.tensor.matmul(ps[:, y_bank0 + u, t * P:(t + 1) * P],
                                                     hT[:, u, f, t * P:(t + 1) * P], w2[:, f, :],
                                                     start=(f == 0), stop=(f == FB - 1))
                        i.then_inc(s_y, 1)

                    pe.wait_ge(s_w, 1 + BASE)
                    run_chunks(pe, body, (turn,))

                @block.scalar
                def _(act):
                    act.sem_inc(s_gl, FB)

                    def copy_turned(b, u):
                        act.wait_ge(s_T, 2 * b + u + 1 + BASE)
                        act.wait_ge(s_h, FB * (2 * b + u) + 1 + BASE)
                        nc.scalar.activation(xnT[:, u, :], ps[:, u, :], ACT.Copy).then_inc(s_xT, 1)

                    def body(b, u, ahead):
                        act.wait_ge(s_y, 2 * b + u + 1 + BASE)
                        for f in range(FB):
                            act.wait_ge(s_h, FB * (2 * b + u + 1) + f + 2 + BASE)
                            nc.scalar.activation(hT[:, u, f, :], ps[:, h_bank0 + f, :], ACT.Gelu_apprx_tanh,
                                                 bias=w_sb["b1"][:, f:f + 1]).then_inc(s_gl, 1)
                        if ahead is not None:
                            copy_turned(*ahead)

                    run_chunks(act, body, (copy_turned,))

                @block.sync
                def _(sp):
                    def body(b, u, ahead):
                        sp.wait_ge(s_res, 2 * b + u + 1 + BASE)
                        sp.dma_start(out.rearrange("b (t p) c -> p (b t) c", p=P)
                                     [:, bass.ds((b * HALVES + u) * CT, CT), :],
                                     tiles_of(x_res, b, u)).then_inc(s_st[u], 16)

                    run_chunks(sp, body)
                    for u in range(2):
                        sp.wait_ge(s_st[u], 16 * BATCH + BASE)

        end_phase()
        project_heads8("p0", w_sb["wq0"][:, :], w_sb["wk0"][:, :], w_sb["wv0"][:, :])
        end_phase()
        attention("a0", 8.0 ** -0.5, latent=False, has_max=False, clip=True)
        end_phase()
        finish_heads8("f0", w_sb["wout0"][:, :])
        end_phase()
        project_latent()
        end_phase()
        attention("am", 0.125, latent=True, has_max=True, clip=False)
        end_phase()
        finish_latent()
        end_phase()
        experts()
        end_phase()
        project_heads8("p1", w_sb["wq1"][:, :], w_sb["wk1"][:, :], w_sb["wv1"][:, :])
        end_phase()
        attention("a1", 8.0 ** -0.5, latent=False, has_max=True, clip=False)
        end_phase()
        finish_heads8("f1", None)
        end_phase()
        low_rank_ffn()
        end_phase()


def lay_out(inputs):
    a = {k: np.asarray(v) for k, v in inputs.items()}
    f = np.float32
    order = np.arange(C).reshape(NQ, 2, 2, 8).transpose(0, 2, 3, 1).reshape(-1)
    w0, w1 = a["L0_attn_Wqkv"].T, a["L1_attn_w_qkv"]
    c = {
        "wq0": w0[:, 0:C][:, order], "wk0": w0[:, C:2 * C][:, order], "wv0": w0[:, 2 * C:],
        "wq1": w1[:, 0:C][:, order], "wk1": w1[:, C:2 * C][:, order], "wv1": w1[:, 2 * C:],
        "wout0": a["L0_attn_Wout"].T,
    }
    wq = a["L0_ffn_Wq"].reshape(C, HEADS, 64)
    c["wq_nope"] = wq[:, :, 0:32].transpose(2, 1, 0)
    rope = wq[:, :, 32:].reshape(C, NQ, QUAD, 32).transpose(0, 1, 3, 2)
    swap = np.arange(32).reshape(16, 2)[:, ::-1].reshape(-1)
    c["wq_rope"] = rope.reshape(C, NQ, P)
    c["wq_rope_sw"] = rope[:, :, swap].reshape(C, NQ, P)
    c["wkva"] = a["L0_ffn_Wkva"]
    c["wkva_sw"] = np.concatenate([a["L0_ffn_Wkva"][:, 0:LAT], a["L0_ffn_Wkva"][:, LAT + swap]], axis=1)
    wkvb = a["L0_ffn_Wkvb"].reshape(LAT, HEADS, 32)
    z = np.zeros((32, HEADS, P), f)
    for h in range(HEADS):
        z[:, h, (h % 8) * LAT:(h % 8 + 1) * LAT] = wkvb[:, h].T
    c["wkvb_z"] = z
    c["wo_nope"] = a["L0_ffn_Wo"].reshape(HEADS, 64, C)[:, 0:32].transpose(1, 0, 2)
    c["ln1"] = a["L0_ffn_w_ln1"].reshape(C, 1)
    c["ln2"] = a["L0_ffn_w_ln2"].reshape(C, 1)
    c["wgate"] = a["L0_ffn_Wgate"]
    c["bias"] = np.broadcast_to(a["L0_ffn_expert_bias"], (P, EXPERTS))
    c["wg"] = np.concatenate([a["L0_ffn_Wg"], a["L0_ffn_sWg"]]).transpose(1, 0, 2).reshape(C, -1)
    c["wu"] = np.concatenate([a["L0_ffn_Wu"], a["L0_ffn_sWu"]]).transpose(1, 0, 2).reshape(C, -1)
    wd = np.concatenate([a["L0_ffn_Wd"], a["L0_ffn_sWd"]]).reshape(-1, C)
    wd = np.concatenate([wd, np.zeros((INNER, C), f)])
    c["wd"] = wd.reshape(PAIRS + 1, P, C).transpose(1, 0, 2)
    c["u1t"], c["v1"], c["u2t"], c["v2"] = a["L1_ffn_U1"].T, a["L1_ffn_V1"], a["L1_ffn_U2"].T, a["L1_ffn_V2"]
    c["b1"] = a["L1_ffn_b1"].reshape(DFF // P, P).T
    c["b2"] = np.broadcast_to(a["L1_ffn_b2"], (P, C))
    ang = np.outer(np.arange(T, dtype=f), f(1.0) / f(100000.0) ** (np.arange(0, 32, 2, dtype=f) / f(32))).T
    cos, sin = np.repeat(np.cos(ang), 2, 0), np.repeat(np.sin(ang), 2, 0)
    sin[0::2] = -sin[0::2]
    c["cos_q"], c["sin_q"] = np.repeat(cos, QUAD, 0), np.repeat(sin, QUAD, 0)
    c["cos_k"] = np.concatenate([np.ones((LAT, T), f), cos])
    c["sin_k"] = np.concatenate([np.zeros((LAT, T), f), sin])
    e = np.arange(EXPERTS)
    c["earlier"] = np.broadcast_to((e[None, :] < e[:, None]).astype(f).reshape(-1), (P, EXPERTS * EXPERTS))
    c["spread"] = np.repeat(np.eye(EXPERTS, dtype=f), INNER, axis=1)
    return {k: np.ascontiguousarray(v) for k, v in c.items()}


def kernel(**inputs):
    import concourse.bacc as bacc
    from concourse.bass_utils import run_bass_kernel_spmd as run

    nc = bacc.Bacc("TRN2", target_bir_lowering=False, num_devices=1)
    arrays = {"in_x": np.ascontiguousarray(inputs["L0_attn_x"])}
    x = nc.dram_tensor("in_x", arrays["in_x"].shape, F32, kind="ExternalInput").ap()
    consts = {}
    for n, v in lay_out(inputs).items():
        arrays["in_" + n] = v
        consts[n] = nc.dram_tensor("in_" + n, v.shape, F32, kind="ExternalInput").ap()
    out = nc.dram_tensor("out", (BATCH, T, C), F32, kind="ExternalOutput").ap()
    build(nc, {"x": x}, consts, out)
    return run(nc, [arrays], core_ids=[0]).results[0]["out"]
```
